# Optimizing a Trainium2 kernel written in Bass

```python
import numpy as np
import jax
import jax.numpy as jnp

def _softmax(x, axis=-1):
    return jax.nn.softmax(x, axis=axis)

def _gelu(x):
    return jax.nn.gelu(x, approximate=True)

def _silu(x):
    return jax.nn.silu(x)

def _sigmoid(x):
    return jax.nn.sigmoid(x)

def _layernorm(x, axis=-1, eps=1e-05):
    m = jnp.mean(x, axis=axis, keepdims=True)
    v = jnp.var(x, axis=axis, keepdims=True)
    return (x - m) / jnp.sqrt(v + eps)

def _scatter_add(tgt, idx, src, axis=0):
    return tgt.at[idx].add(src)

def _segment_sum(src, seg, n):
    return jax.ops.segment_sum(src, seg, n)
kernel_name = 'mk_adj_resnorm_d2_adj_r2_dde396'

def setup_inputs(seed: int=0):
    np.random.seed(seed)
    _w = jnp.asarray

    def _rec_inputs():
        import jax
        import jax.numpy as jnp
        _gk = jax.random.key(seed)
        x = -0.0005207 + 1.001 * jax.random.normal(jax.random.fold_in(_gk, 1), (8192, 128), jnp.float32)
        _a = jax.random.bernoulli(jax.random.fold_in(_gk, 2), 0.000488281, (8192, 8192))
        _a = jnp.logical_or(_a, jnp.eye(8192, dtype=bool))
        _af = _a.astype(jnp.float32)
        _af = _af * jax.random.uniform(jax.random.fold_in(_gk, 3), (8192, 8192), jnp.float32, 0.05, 1)
        adj = _af
        return (x, adj)
    x, adj = _rec_inputs()

    def _L0_gnn_setup():
        import jax, jax.numpy as jnp
        import numpy as np
        ALPHA = 0.1
        N, F = (8192, 128)
        key = jax.random.key(seed)
        k1, k2, k3 = jax.random.split(key, 3)
        x = jax.random.normal(k1, (N, F), dtype=jnp.float32)
        adj = jax.random.uniform(k2, (N, N), dtype=jnp.float32)
        h = jax.random.normal(k3, (N, F), dtype=jnp.float32)
        return {'x': x, 'adj': adj, 'h': h}
    _L0_gnn_all = _L0_gnn_setup()
    _L0_gnn_in = {k: v for k, v in _L0_gnn_all.items() if k in ('h',)}
    del _L0_gnn_all

    def _L1_gnn_setup():
        import jax, jax.numpy as jnp
        import numpy as np
        N, IN_DIM, OUT_DIM = (4096, 128, 128)
        key = jax.random.key(seed)
        k1, k2, k3, k4 = jax.random.split(key, 4)
        X = jax.random.normal(k1, (N, IN_DIM), dtype=jnp.float32)
        A = jax.random.uniform(k2, (N, N), dtype=jnp.float32)
        bound = 1.0 / np.sqrt(IN_DIM)
        W = jax.random.uniform(k3, (OUT_DIM, IN_DIM), minval=-bound, maxval=bound, dtype=jnp.float32)
        b = jax.random.uniform(k4, (OUT_DIM,), minval=-bound, maxval=bound, dtype=jnp.float32)
        return {'X': X, 'A': A, 'W': W, 'b': b}
    _L1_gnn_all = _L1_gnn_setup()
    _L1_gnn_in = {k: v for k, v in _L1_gnn_all.items() if k in ('W', 'b')}
    del _L1_gnn_all
    return {'x': x, 'adj': adj, 'L0_gnn_h': _L0_gnn_in['h'], 'L1_gnn_W': _L1_gnn_in['W'], 'L1_gnn_b': _L1_gnn_in['b']}

def reference(x, adj, L0_gnn_h, L1_gnn_W, L1_gnn_b):
    import jax
    import jax.numpy as jnp

    def _L0_gnn_ref(x, adj, h):
        import jax, jax.numpy as jnp
        import numpy as np
        ALPHA = 0.1
        N, F = (8192, 128)
        return (1.0 - ALPHA) * (adj @ x) + ALPHA * h

    def _L1_gnn_ref(X, A, W, b):
        import jax, jax.numpy as jnp
        import numpy as np
        N, IN_DIM, OUT_DIM = (4096, 128, 128)
        n = A.shape[0]
        A_hat = A + jnp.eye(n, dtype=A.dtype)
        d_inv_sqrt = A_hat.sum(axis=1) ** (-0.5)
        A_norm = d_inv_sqrt[:, None] * A_hat * d_inv_sqrt[None, :]
        H = A_norm @ X
        return H @ W.T + b
    x = _layernorm(x + _L0_gnn_ref(x, adj, L0_gnn_h), axis=-1)
    x = _layernorm(x + _L1_gnn_ref(x, adj, L1_gnn_W, L1_gnn_b), axis=-1)
    return x

_drawn_inputs = setup_inputs


def setup_inputs(seed=0):
    import zlib

    import numpy as np

    out = dict(_drawn_inputs(seed))
    spreads = {}
    factors = {}
    for name, (base, spread) in spreads.items():
        noise = np.random.default_rng([zlib.crc32(name.encode()), seed]).standard_normal(out[name].shape)
        drawn = base * np.exp(spread * noise) if base else spread * noise
        out[name] = jnp.asarray(drawn.astype(out[name].dtype))
    for name, factor in factors.items():
        out[name] = (out[name] * factor).astype(out[name].dtype)
    return out
```

```python
import concourse.bass as bass
from concourse import mybir
from contextlib import ExitStack



def graph_resnorm_kernel(nc, x, adj, h, W, b, out):
    fp32 = mybir.dt.float32
    f32r = mybir.dt.float32r
    ALU = mybir.AluOpType
    ACT = mybir.ActivationFunctionType
    AX = mybir.AxisListType

    N, F = x.shape
    P = 128
    ALPHA = 0.1
    EPS = 1e-5
    ROWS = 512
    R = ROWS // P
    BLOCKS = N // ROWS
    JT = N // P
    PAIR = 2
    STEPS = JT // PAIR
    CCOLS = 512
    CHUNKS = N // CCOLS
    SPC = CCOLS // (PAIR * P)
    SLOTS = 4
    HALVES = 4
    FOLD = CCOLS // 2
    HEAD = 2
    XT = JT // SLOTS

    adj_v = adj.rearrange("(n r p) (c k) -> n c p r k", r=R, p=P, k=CCOLS)
    x_v = x.rearrange("(q t p) f -> q p t f", t=XT, p=P)
    h_v = h.rearrange("(n r p) f -> n p r f", r=R, p=P)
    out_v = out.rearrange("(n r p) f -> n p r f", r=R, p=P)
    resid = nc.dram_tensor("resid", (BLOCKS, P, R, F), fp32, kind="Internal").ap()

    ctx = ExitStack()
    with ctx:
        def sb(name, shape, dt=fp32):
            return ctx.enter_context(nc.sbuf_tensor(name, shape, dt))

        def pb(name, shape, dt=fp32):
            return ctx.enter_context(nc.psum_tensor(name, shape, dt))

        def sem(name):
            return ctx.enter_context(nc.semaphore(name))

        x_hi = sb("x_hi", [P, JT, F], f32r)
        x_lo = sb("x_lo", [P, JT, F], f32r)
        u_hi = sb("u_hi", [P, JT, F], f32r)
        u_lo = sb("u_lo", [P, JT, F], f32r)
        chunk = sb("chunk", [P, SLOTS, R, CCOLS])
        a_hi = sb("a_hi", [P, HALVES, PAIR * ROWS], f32r)
        a_lo = sb("a_lo", [P, HALVES, PAIR * ROWS], f32r)
        fold = sb("fold", [P, 2, R, FOLD])
        feat = sb("feat", [P, ROWS])
        rows = sb("rows", [P, R, F])
        ident = sb("ident", [P, P])
        w_t = sb("w_t", [P, F])
        b_bc = sb("b_bc", [P, F])
        partial = sb("partial", [P, R, CHUNKS])
        deg = sb("deg", [P, R])
        sqrt_deg = sb("sqrt_deg", [P, R])
        dinv_all = sb("dinv_all", [P, BLOCKS * R])
        dinv = sb("dinv", [P, R])
        dinv2 = sb("dinv2", [P, R])
        stats = sb("stats", [P, R, 6])
        mv = sb("mv", [P, R, 2])
        std = sb("std", [P, R])
        rstd = sb("rstd", [P, R])
        carrier = sb("carrier", [P, 1])

        a_t = [pb(f"a_t{i}", [P, PAIR * ROWS]) for i in range(2)]
        acc_head = pb("acc_head", [P, ROWS])
        acc_tail = pb("acc_tail", [P, ROWS])
        row_ps = pb("row_ps", [P, ROWS])
        x1_ps = pb("x1_ps", [P, ROWS])

        loaded = [sem(f"loaded{i}") for i in range(SLOTS)]
        w_loaded = sem("w_loaded")
        b_loaded = sem("b_loaded")
        ident_ready = sem("ident_ready")
        ident_zero = sem("ident_zero")
        w_trans = sem("w_trans")
        w_ready = sem("w_ready")
        xh_ready = sem("xh_ready")
        xl_ready = sem("xl_ready")
        transposed = sem("transposed")
        hi_ready = sem("hi_ready")
        lo_ready = sem("lo_ready")
        multiplied = sem("multiplied")
        folded = sem("folded")
        sums_act = sem("sums_act")
        sums_dve = sem("sums_dve")
        deg_ready = sem("deg_ready")
        sqrt_ready = sem("sqrt_ready")
        dinv_ready = sem("dinv_ready")
        head_out = sem("head_out")
        tail_out = sem("tail_out")
        y_ready = sem("y_ready")
        rows_loaded = sem("rows_loaded")
        var_ready = sem("var_ready")
        std_ready = sem("std_ready")
        x1_ready = sem("x1_ready")
        x1_trans = sem("x1_trans")
        x1t_ready = sem("x1t_ready")
        p_ready = sem("p_ready")
        uh_ready = sem("uh_ready")
        ul_ready = sem("ul_ready")
        rows_done = sem("rows_done")
        rows_stored = sem("rows_stored")
        mv_ready = sem("mv_ready")
        rstd_ready = sem("rstd_ready")
        bias_added = sem("bias_added")
        chain = sem("chain")

        block = ctx.enter_context(nc.Block())

        LAST = 2 * BLOCKS - 1


        @block.sync
        def _(sp):
            for q in range(SLOTS):
                sp.dma_start(chunk[:, q, :, :].rearrange("p r (t f) -> p (r t) f", f=F),
                             x_v[q]).then_inc(loaded[q], 16)
            sp.dma_start(feat[:, 0:F], W[:, :]).then_inc(w_loaded, 16)
            sp.dma_start(b_bc[:, :], b.rearrange("(o f) -> o f", o=1).broadcast_to([P, F])).then_inc(b_loaded, 16)

            def load_rows(g, row_block, source):
                sp.dma_start(rows[:, :, :], source[row_block]).then_inc(rows_loaded, 16)

            def store_rows(g, row_block, target):
                sp.wait_ge(rows_done, 16 * g)
                sp.dma_start(target[row_block], rows[:, :, :]).then_inc(rows_stored, 16)

            def rows_free(g):
                sp.wait_ge(rows_stored, 16 * g)

            def run_block(g, row_block, sums, done):
                for c in range(CHUNKS):
                    if isinstance(g, int) and g == 0 and c < SLOTS:
                        sp.wait_ge(xl_ready, c + 1)
                    else:
                        gone = g * STEPS + (c - SLOTS + 1) * SPC
                        sp.wait_ge(transposed, gone)
                        if sums or c < SLOTS:
                            sp.wait_ge(folded, gone)
                    if c == 2 and done is not None:
                        load_rows(g, *done[0:2])
                    if c == CHUNKS - 1 and done is not None:
                        rows_free(g)
                    sp.dma_start(chunk[:, c % SLOTS, :, :], adj_v[row_block, c]).then_inc(loaded[c % SLOTS], 16)
                    if c == CHUNKS - 3 and done is not None:
                        store_rows(g, done[0], done[2])

            run_block(0, 0, True, None)
            with sp.Fori(1, BLOCKS) as g:
                run_block(g, g, True, (g - 1, h_v, resid))
            run_block(BLOCKS, 0, False, (BLOCKS - 1, h_v, resid))
            with sp.Fori(BLOCKS + 1, 2 * BLOCKS) as g:
                sp_rows = g - BLOCKS - 1
                for c in range(CHUNKS):
                    sp.wait_ge(transposed, g * STEPS + (c - SLOTS + 1) * SPC)
                    if c == 2:
                        load_rows(g, sp_rows, resid)
                    if c == CHUNKS - 1:
                        rows_free(g)
                    sp.dma_start(chunk[:, c % SLOTS, :, :], adj_v[g - BLOCKS, c]).then_inc(loaded[c % SLOTS], 16)
                    if c == CHUNKS - 3:
                        store_rows(g, sp_rows, out_v)
            load_rows(2 * BLOCKS, BLOCKS - 1, resid)
            store_rows(2 * BLOCKS, BLOCKS - 1, out_v)
            rows_free(2 * BLOCKS)

        @block.gpsimd
        def _(pool):
            nc.gpsimd.memset(ident[:, :], 0.0).then_inc(ident_zero, 1)
            pool.wait_ge(ident_zero, 1)
            nc.gpsimd.affine_select(out=ident[:, :], in_=ident[:, :], compare_op=ALU.not_equal, fill=1.0,
                                    base=0, pattern=[[-1, P]], channel_multiplier=1).then_inc(ident_ready, 1)

            def fold_block(g):
                for c in range(CHUNKS):
                    pool.wait_ge(loaded[c % SLOTS], 16 * (g * (CHUNKS // SLOTS) + c // SLOTS + 2))
                    if not (isinstance(g, int) and g == 0 and c < 2):
                        pool.wait_ge((sums_act, sums_dve)[c % 2], g * (CHUNKS // 2) + c // 2)
                    nc.gpsimd.tensor_tensor(fold[:, c % 2, :, :], chunk[:, c % SLOTS, :, 0:FOLD],
                                            chunk[:, c % SLOTS, :, FOLD:CCOLS], ALU.add).then_inc(folded, SPC)

            fold_block(0)
            with pool.Fori(1, BLOCKS) as g:
                fold_block(g)

        @block.tensor
        def _(pe):
            def transpose_step(g, s):
                if s % SPC == 0:
                    c = s // SPC
                    pe.wait_ge(loaded[c % SLOTS], 16 * (g * (CHUNKS // SLOTS) + c // SLOTS + 2))
                if not (isinstance(g, int) and g == 0 and s < 2):
                    pe.wait_ge(lo_ready, g * STEPS + s - 1)
                for t in range(PAIR):
                    col = (s % SPC * PAIR + t) * P
                    for r in range(R):
                        last = nc.tensor.transpose(a_t[s % 2][:, (t * R + r) * P:(t * R + r + 1) * P],
                                                   chunk[:, s // SPC % SLOTS, r, col:col + P], ident[:, :])
                last.then_inc(transposed, 1)

            def multiply_step(g, s, hi, lo, ahead):
                acc = acc_head if s < HEAD else acc_tail
                first, final = s in (0, HEAD), s in (HEAD - 1, STEPS - 1)
                pe.wait_ge(hi_ready, g * STEPS + s + 1)
                for t in range(PAIR):
                    moving = a_hi[:, s % HALVES, t * ROWS:(t + 1) * ROWS]
                    nc.tensor.matmul(acc[:, :], hi[:, s * PAIR + t, :], moving, start=first and t == 0, stop=False)
                    nc.tensor.matmul(acc[:, :], lo[:, s * PAIR + t, :], moving, start=False, stop=False)
                if ahead is not None:
                    transpose_step(*ahead)
                pe.wait_ge(lo_ready, g * STEPS + s + 1)
                for t in range(PAIR):
                    last = nc.tensor.matmul(acc[:, :], hi[:, s * PAIR + t, :],
                                            a_lo[:, s % HALVES, t * ROWS:(t + 1) * ROWS],
                                            start=False, stop=final and t == PAIR - 1)
                last.then_inc(multiplied, 1)

            def rows_back(g):
                pe.wait_ge(tail_out, g)
                for r in range(R):
                    last = nc.tensor.transpose(row_ps[:, r * P:(r + 1) * P], feat[:, r * P:(r + 1) * P], ident[:, :])
                last.then_inc(y_ready, 1)

            def x1_transpose(g):
                pe.wait_ge(x1_ready, g)
                for r in range(R):
                    last = nc.tensor.transpose(x1_ps[:, r * P:(r + 1) * P], rows[:, r, :], ident[:, :])
                last.then_inc(x1_trans, 1)

            def x1_weights(g):
                pe.wait_ge(x1t_ready, g)
                for r in range(R):
                    last = nc.tensor.matmul(row_ps[:, r * P:(r + 1) * P], feat[:, r * P:(r + 1) * P], w_t[:, :],
                                            start=True, stop=True)
                last.then_inc(p_ready, 1)

            def run_block(g, hi, lo, row_work, u_here, ahead_of_next):
                for s in range(STEPS):
                    if isinstance(g, int) and g == 0 and s % (XT // PAIR) == 0:
                        pe.wait_ge(xl_ready, s // (XT // PAIR) + 1)
                    if u_here and s == 0:
                        pe.wait_ge(ul_ready, BLOCKS - 1)
                    if u_here and s == STEPS - R // PAIR:
                        pe.wait_ge(ul_ready, BLOCKS)
                    if row_work and s == 0:
                        pe.wait_ge(head_out, g)
                    if row_work and s == HEAD:
                        pe.wait_ge(tail_out, g)
                    if s + 2 < STEPS:
                        ahead = (g, s + 2)
                    else:
                        ahead = (g + 1, s + 2 - STEPS) if ahead_of_next else None
                    multiply_step(g, s, hi, lo, ahead)
                    if row_work and s == 2:
                        rows_back(g)
                    if row_work == "first" and s == 11:
                        x1_transpose(g)
                    if row_work == "first" and s == 14:
                        x1_weights(g)

            pe.wait_ge(ident_ready, 1)
            pe.wait_ge(w_loaded, 16)
            nc.tensor.transpose(row_ps[:, 0:F], feat[:, 0:F], ident[:, :]).then_inc(w_trans, 1)
            pe.wait_ge(w_ready, 1)
            transpose_step(0, 0)
            transpose_step(0, 1)
            run_block(0, x_hi, x_lo, None, False, True)
            with pe.Fori(1, BLOCKS) as g:
                run_block(g, x_hi, x_lo, "first", False, True)
            run_block(BLOCKS, u_hi, u_lo, "first", True, True)
            with pe.Fori(BLOCKS + 1, LAST) as g:
                run_block(g, u_hi, u_lo, "second", False, True)
            run_block(LAST, u_hi, u_lo, "second", False, False)
            rows_back(LAST + 1)

        @block.scalar
        def _(act):
            def take_hi(g, s):
                act.wait_ge(transposed, g * STEPS + s + 1)
                if not (isinstance(g, int) and g == 0 and s < HALVES):
                    act.wait_ge(multiplied, g * STEPS + s - HALVES + 1)
                nc.scalar.activation(a_hi[:, s % HALVES, :], a_t[s % 2][:, :], ACT.Copy).then_inc(hi_ready, 1)

            def sum_chunk(g, c, part):
                act.wait_ge(folded, g * STEPS + (c + 1) * SPC)
                if c == 0 and part == 0 and not (isinstance(g, int) and g == 0):
                    act.wait_ge(deg_ready, g)
                for r in (2 * part, 2 * part + 1):
                    last = nc.scalar.activation(fold[:, c % 2, r, :], fold[:, c % 2, r, :], ACT.Copy,
                                                accum_out=partial[:, r, c:c + 1])
                if part == 1:
                    last.then_inc(sums_act, 1)

            def root_degrees(g):
                act.wait_ge(deg_ready, g)
                nc.scalar.activation(sqrt_deg[:, :], deg[:, :], ACT.Sqrt).then_inc(sqrt_ready, 1)

            def deviation(g):
                act.wait_ge(var_ready, g)
                nc.scalar.activation(std[:, :], std[:, :], ACT.Sqrt).then_inc(std_ready, 1)

            def x1_copy(g):
                act.wait_ge(x1_trans, g)
                nc.scalar.activation(feat[:, :], x1_ps[:, :], ACT.Copy).then_inc(x1t_ready, 1)

            def u_high(g, row_block):
                act.wait_ge(p_ready, g)
                act.wait_ge(dinv_ready, g)
                for r in range(R):
                    last = nc.scalar.activation(u_hi[:, row_block * R + r, :], row_ps[:, r * P:(r + 1) * P], ACT.Copy,
                                                scale=dinv[:, r:r + 1])
                last.then_inc(uh_ready, 1)

            def take_head(g):
                act.wait_ge(multiplied, g * STEPS + HEAD)
                nc.scalar.activation(feat[:, :], acc_head[:, :], ACT.Copy).then_inc(head_out, 1)

            def run_block(g, row_work, sums):
                for s in range(STEPS):
                    take_hi(g, s)
                    if sums and s >= SPC and (s // SPC - 1) % 2 == 0:
                        sum_chunk(g, s // SPC - 1, s % SPC)
                    if row_work == "first" and s == 2:
                        root_degrees(g)
                    if row_work and s == 8:
                        deviation(g)
                    if row_work == "first" and s == 13:
                        x1_copy(g)
                    if row_work == "first" and s == 16:
                        u_high(g, g - 1)
                    if s == 20:
                        if row_work == "first":
                            act.wait_ge(p_ready, g)
                        elif row_work:
                            act.wait_ge(y_ready, g)
                        take_head(g)

            for q in range(SLOTS):
                act.wait_ge(loaded[q], 16)
                nc.scalar.activation(x_hi[:, q * XT:(q + 1) * XT, :],
                                     chunk[:, q, :, :].rearrange("p r (t f) -> p (r t) f", f=F),
                                     ACT.Copy).then_inc(xh_ready, 1)
                if q == 0:
                    act.wait_ge(w_trans, 1)
                    nc.scalar.activation(w_t[:, :], row_ps[:, 0:F], ACT.Copy).then_inc(w_ready, 1)
            run_block(0, None, True)
            with act.Fori(1, BLOCKS) as g:
                run_block(g, "first", True)
            run_block(BLOCKS, "first", False)
            with act.Fori(BLOCKS + 1, 2 * BLOCKS) as g:
                run_block(g, "second", False)
            deviation(LAST + 1)

        @block.vector
        def _(dve):
            CH1, CH2 = 5, 3

            def link(ins):
                return ins.then_inc(chain, 1)

            def take_lo(g, s):
                dve.wait_ge(hi_ready, g * STEPS + s + 1)
                nc.vector.tensor_tensor(a_lo[:, s % HALVES, :], a_t[s % 2][:, :],
                                        a_hi[:, s % HALVES, :].bitcast(fp32), ALU.subtract).then_inc(lo_ready, 1)

            def sum_chunk(g, c, part):
                dve.wait_ge(folded, g * STEPS + (c + 1) * SPC)
                last = nc.vector.tensor_reduce(partial[:, 2 * part:2 * part + 2, c:c + 1],
                                               fold[:, c % 2, 2 * part:2 * part + 2, :], AX.X, ALU.add)
                if part == 1:
                    last.then_inc(sums_dve, 1)

            def degrees(g, base):
                dve.wait_ge(sums_act, g * (CHUNKS // 2))
                dve.wait_ge(sums_dve, g * (CHUNKS // 2))
                link(nc.vector.tensor_reduce(deg[:, :], partial[:, :, :], AX.X, ALU.add))
                dve.wait_ge(chain, base + 1)
                nc.vector.tensor_scalar(deg[:, :], deg[:, :], 1.0, None, ALU.add).then_inc(deg_ready, 1)

            def inverse_degrees(g, row_block):
                dve.wait_ge(sqrt_ready, g)
                nc.vector.reciprocal(dinv[:, :], sqrt_deg[:, :])
                nc.vector.reciprocal(dinv_all[:, bass.ds(row_block * R, R)], sqrt_deg[:, :])
                nc.vector.reciprocal(dinv2[:, :], deg[:, :]).then_inc(dinv_ready, 1)

            def add_tail(g):
                dve.wait_ge(multiplied, g * STEPS)
                dve.wait_ge(head_out, g)
                nc.vector.tensor_tensor(feat[:, :], acc_tail[:, :], feat[:, :], ALU.add).then_inc(tail_out, 1)

            def mix_inputs(g, row_block, base):
                dve.wait_ge(rows_loaded, 16 * g)
                tiles = bass.ds(row_block * R, R)
                link(nc.vector.scalar_tensor_tensor(rows[:, :, :], rows[:, :, :], ALPHA,
                                                    x_hi[:, tiles, :].bitcast(fp32), ALU.mult, ALU.add))
                dve.wait_ge(chain, base + 2)
                link(nc.vector.tensor_tensor(rows[:, :, :], rows[:, :, :], x_lo[:, tiles, :].bitcast(fp32), ALU.add))

            def first_rows(g, base):
                dve.wait_ge(y_ready, g)
                dve.wait_ge(chain, base + 3)
                link(nc.vector.scalar_tensor_tensor(rows[:, :, :], row_ps[:, :].rearrange("p (r f) -> p r f", f=F),
                                                    1.0 - ALPHA, rows[:, :, :], ALU.mult, ALU.add))

            def second_rows(g):
                dve.wait_ge(y_ready, g)
                dve.wait_ge(rows_loaded, 16 * g)
                for r in range(R):
                    last = nc.vector.scalar_tensor_tensor(rows[:, r, :], row_ps[:, r * P:(r + 1) * P],
                                                          dinv[:, r:r + 1], rows[:, r, :], ALU.mult, ALU.add)
                link(last)

            def statistics(seen):
                dve.wait_ge(chain, seen)
                for r in range(R):
                    last = nc.vector.bn_stats(stats[:, r, :], rows[:, r, :])
                link(last)

            def variance(seen):
                dve.wait_ge(chain, seen)
                nc.vector.memset(carrier[:, :], 0.0)
                for r in range(R):
                    last = nc.vector.bn_aggr(mv[:, r, :], stats[:, r, :])
                last.then_inc(mv_ready, 1)

            def add_eps(g):
                dve.wait_ge(mv_ready, g)
                nc.vector.tensor_scalar(std[:, :], mv[:, :, 1], EPS, None, ALU.add).then_inc(var_ready, 1)

            def inverse_deviation(g):
                dve.wait_ge(std_ready, g)
                nc.vector.reciprocal(rstd[:, :], std[:, :]).then_inc(rstd_ready, 1)

            def normalise(g, done, by):
                dve.wait_ge(rstd_ready, g)
                for r in range(R):
                    last = nc.vector.tensor_scalar(rows[:, r, :], rows[:, r, :], mv[:, r, 0:1], rstd[:, r:r + 1],
                                                   ALU.subtract, ALU.mult)
                last.then_inc(done, by)

            def u_low(g, row_block):
                dve.wait_ge(uh_ready, g)
                for r in range(R):
                    last = nc.vector.scalar_tensor_tensor(u_lo[:, row_block * R + r, :], row_ps[:, r * P:(r + 1) * P],
                                                          dinv[:, r:r + 1],
                                                          u_hi[:, row_block * R + r, :].bitcast(fp32),
                                                          ALU.mult, ALU.subtract)
                last.then_inc(ul_ready, 1)

            def residual_bias(g):
                dve.wait_ge(x1_trans, g)
                bias = b_bc[:, :].rearrange("p (o f) -> p o f", o=1).broadcast_to([P, R, F])
                nc.vector.tensor_tensor(rows[:, :, :], rows[:, :, :], bias, ALU.add).then_inc(bias_added, 1)

            def residual(g):
                dve.wait_ge(bias_added, g)
                dve.wait_ge(p_ready, g)
                for r in range(R):
                    last = nc.vector.scalar_tensor_tensor(rows[:, r, :], row_ps[:, r * P:(r + 1) * P],
                                                          dinv2[:, r:r + 1], rows[:, r, :], ALU.mult, ALU.add)
                last.then_inc(rows_done, 16)

            def run_block(g, row_work, sums):
                base = None
                if row_work == "first":
                    base = (g - 1) * CH1
                if row_work == "second":
                    base = BLOCKS * CH1 + (g - BLOCKS - 1) * CH2
                for s in range(STEPS):
                    take_lo(g, s)
                    if sums and s >= SPC and (s // SPC - 1) % 2 == 1:
                        sum_chunk(g, s // SPC - 1, s % SPC)
                    if row_work == "first":
                        if s < 2:
                            sum_chunk(g - 1, CHUNKS - 1, s)
                        if s == 1:
                            add_tail(g)
                            degrees(g, base)
                        if s == 3:
                            inverse_degrees(g, g - 1)
                        if s == 4:
                            mix_inputs(g, g - 1, base)
                        if s == 5:
                            first_rows(g, base)
                        if s == 6:
                            statistics(base + 4)
                        if s == 7:
                            variance(base + 5)
                            add_eps(g)
                        if s == 9:
                            inverse_deviation(g)
                        if s == 10:
                            normalise(g, x1_ready, 1)
                        if s == 15:
                            residual_bias(g)
                        if s == 17:
                            u_low(g, g - 1)
                        if s == 18:
                            residual(g)
                    if row_work == "second":
                        if s == 1:
                            add_tail(g)
                        if s == 3:
                            take_dinv(g - 1 - BLOCKS, base)
                        if s == 5:
                            dve.wait_ge(chain, base + 1)
                            second_rows(g)
                        if s == 6:
                            statistics(base + 2)
                        if s == 7:
                            variance(base + 3)
                            add_eps(g)
                        if s == 9:
                            inverse_deviation(g)
                        if s == 10:
                            normalise(g, rows_done, 16)

            def take_dinv(row_block, base):
                link(nc.vector.tensor_copy(dinv[:, :], dinv_all[:, bass.ds(row_block * R, R)]))

            for q in range(SLOTS):
                dve.wait_ge(xh_ready, q + 1)
                nc.vector.tensor_tensor(x_lo[:, q * XT:(q + 1) * XT, :],
                                        chunk[:, q, :, :].rearrange("p r (t f) -> p (r t) f", f=F),
                                        x_hi[:, q * XT:(q + 1) * XT, :].bitcast(fp32),
                                        ALU.subtract).then_inc(xl_ready, 1)
            dve.wait_ge(b_loaded, 16)
            run_block(0, None, True)
            with dve.Fori(1, BLOCKS) as g:
                run_block(g, "first", True)
            run_block(BLOCKS, "first", False)
            with dve.Fori(BLOCKS + 1, 2 * BLOCKS) as g:
                run_block(g, "second", False)
            last_base = BLOCKS * CH1 + (LAST - BLOCKS) * CH2
            add_tail(LAST + 1)
            take_dinv(BLOCKS - 1, last_base)
            dve.wait_ge(chain, last_base + 1)
            second_rows(LAST + 1)
            statistics(last_base + 2)
            variance(last_base + 3)
            add_eps(LAST + 1)
            inverse_deviation(LAST + 1)
            normalise(LAST + 1, rows_done, 16)


_INS = ["x", "adj", "L0_gnn_h", "L1_gnn_W", "L1_gnn_b"]


def kernel(**inputs):
    import numpy as _np
    import concourse.bacc as _bacc
    from concourse import mybir as _mybir
    from concourse.bass_utils import run_bass_kernel_spmd as _run

    nc = _bacc.Bacc("TRN2", target_bir_lowering=False, num_devices=1)
    arrays, args = {}, []
    for name in _INS:
        a = _np.ascontiguousarray(inputs[name])
        arrays[f"in_{name}_dram"] = a
        args.append(nc.dram_tensor(f"in_{name}_dram", a.shape, _mybir.dt.from_np(a.dtype), kind="ExternalInput").ap())
    shape = tuple(inputs["x"].shape)
    args.append(nc.dram_tensor("out_dram", shape, _mybir.dt.float32, kind="ExternalOutput").ap())
    graph_resnorm_kernel(nc, *args)
    r = _run(nc, [arrays], core_ids=[0])
    return r.results[0]["out_dram"]
```

```python
import concourse.bass as bass
from concourse import mybir
from contextlib import ExitStack



def plan(kinds):
    steps, chunks, count, opened = [], [], {"D": 0, "P": 0}, {}
    for s, kind in enumerate(kinds):
        n = count[kind]
        count[kind] += 1
        if n % 2 == 0:
            opened[kind] = len(chunks)
            chunks.append((kind, n // 2, None))
        c = opened[kind]
        chunks[c] = (kind, n // 2, s)
        steps.append((kind, n, c, n % 2))
    return steps, chunks


FIRST_PASS = plan("DP" * 16)
SECOND_PASS = plan("DPDPDDDPDDDPDDDPDDDPDDDPDDDPDDPP")


def graph_resnorm_kernel(nc, x, adj, h, W, b, out):
    fp32 = mybir.dt.float32
    f32r = mybir.dt.float32r
    bf16 = mybir.dt.bfloat16
    ALU = mybir.AluOpType
    ACT = mybir.ActivationFunctionType
    AX = mybir.AxisListType

    N, F = x.shape
    P = 128
    Q = 32
    QN = P // Q
    ALPHA = 0.1
    EPS = 1e-5
    ROWS = 512
    R = ROWS // P
    RB = ROWS // Q
    BLOCKS = N // ROWS
    PAIR = 2
    JT = N // P
    STEPS = JT // PAIR
    SPC = 2
    CCOLS = SPC * PAIR * P
    QCOLS = CCOLS // QN
    CHUNKS = N // CCOLS
    SLOTS = 8
    HIS, LOS, TRS = 8, 4, 4
    HEAD = 2
    LEAD_D, LEAD_P, LEAD_HI, LEAD_LO = 5, 4, 3, 2
    PARTS = 4
    XT = JT // PARTS
    PART_ORDER = (0, 2, 1, 3)
    ALL = 2 * BLOCKS
    PASSES = (FIRST_PASS, SECOND_PASS)
    ND = [sum(s[0] == "D" for s in p[0]) for p in PASSES]
    NP = [STEPS - n for n in ND]
    NPT = [PAIR * n for n in NP]
    DCH = [n // SPC for n in ND]
    PCH = [n // SPC for n in NP]
    DQ = [n * QCOLS for n in DCH]
    DCOLS = [QN * n for n in DQ]
    FOLD = QCOLS // 2
    HALF = RB // 2

    adj_p = adj.rearrange("(n r p) m -> n p r m", r=R, p=P)
    adj_d = adj.rearrange("(n b c) m -> n c b m", b=RB, c=Q)
    x_v = x.rearrange("(n r p) f -> n p r f", r=R, p=P)
    h_v = h.rearrange("(n r p) f -> n p r f", r=R, p=P)
    out_v = out.rearrange("(n r p) f -> n p r f", r=R, p=P)
    resid = nc.dram_tensor("resid", (BLOCKS, P, R, F), fp32, kind="Internal").ap()
    u_dram = nc.dram_tensor("u_dram", (N, F), fp32, kind="Internal").ap()
    u_v = u_dram.rearrange("(n r p) f -> n p r f", r=R, p=P)

    def per_slot(k):
        return 16 * QN if k == "D" else 16

    SLOT_INC = [[sum(per_slot(c[0]) for c in p[1][i::SLOTS]) for i in range(SLOTS)] for p in PASSES]

    def base(g, counts, ps):
        if ps == 0:
            return g * counts[0]
        return g * counts[1] + BLOCKS * (counts[0] - counts[1])

    def stationary(ps, s):
        kind, n, _, _ = PASSES[ps][0][s]
        return PAIR * n if kind == "D" else PAIR * (ND[ps] + n)

    def ahead(g, t, lead, ps):
        u = t + lead
        if u < 0 or isinstance(g, int) and g * STEPS + u >= ALL * STEPS:
            return None
        if u >= STEPS:
            return g + 1, u - STEPS, PASSES[ps][0][u - STEPS]
        return g, u, PASSES[ps][0][u]

    def used_before(g, n, ring, counts, ps):
        if n >= ring:
            return base(g, counts, ps) + n - ring + 1
        before = counts[0 if isinstance(g, int) and g == BLOCKS else ps]
        last = max(m for m in range(before) if m % ring == n)
        return base(g, counts, ps) - before + last + 1

    def in_first(g, n):
        return isinstance(g, int) and g == 0 and n < 0

    ctx = ExitStack()
    with ctx:
        def sb(name, shape, dt=fp32):
            return ctx.enter_context(nc.sbuf_tensor(name, shape, dt))

        def pb(name, shape, dt=fp32):
            return ctx.enter_context(nc.psum_tensor(name, shape, dt))

        def sem(name):
            return ctx.enter_context(nc.semaphore(name))

        s_hi = sb("s_hi", [P, JT, F], f32r)
        s_lo = sb("s_lo", [P, JT, F], f32r)
        chunk = sb("chunk", [P, SLOTS, R * CCOLS])
        a_tr = sb("a_tr", [P, TRS, PAIR * ROWS])
        a_hi = sb("a_hi", [P, HIS, PAIR * ROWS], f32r)
        a_lo = sb("a_lo", [P, LOS, PAIR * ROWS], f32r)
        fold = sb("fold", [P, RB, FOLD])
        feat = sb("feat", [P, ROWS])
        rows = sb("rows", [P, R, F])
        rows2 = sb("rows2", [P, R, F])
        unused = sb("unused", [P, CCOLS], bf16)
        ident = sb("ident", [P, P])
        spread = sb("spread", [P, (2 * QN - 1) * Q])
        w_t = sb("w_t", [P, F])
        b_bc = sb("b_bc", [P, F])
        part_p = sb("part_p", [P, R, PCH[0]])
        part_d = sb("part_d", [P, RB, DCH[0]])
        sum_d = sb("sum_d", [P, RB])
        sum_p = sb("sum_p", [P, R])
        deg = sb("deg", [P, R])
        sqrt_deg = sb("sqrt_deg", [P, R])
        dinv_all = sb("dinv_all", [P, BLOCKS * R])
        dinv = sb("dinv", [P, R])
        dinv2 = sb("dinv2", [P, R])
        stats = sb("stats", [P, R, 6])
        mv = sb("mv", [P, R, 2])
        std = sb("std", [P, R])
        rstd = sb("rstd", [P, R])
        carrier = sb("carrier", [P, 1])

        a_ps = [pb(f"a_ps{i}", [P, PAIR * ROWS]) for i in range(2)]
        acc_head = pb("acc_head", [P, ROWS])
        acc_tail = pb("acc_tail", [P, ROWS])
        row_ps = pb("row_ps", [P, ROWS])
        x1_ps = pb("x1_ps", [P, ROWS])

        loaded = [sem(f"loaded{i}") for i in range(SLOTS)]
        staged = [sem(f"staged{i}") for i in range(PARTS)]
        w_loaded = sem("w_loaded")
        b_loaded = sem("b_loaded")
        zeroed = sem("zeroed")
        consts_ready = sem("consts_ready")
        w_trans = sem("w_trans")
        w_ready = sem("w_ready")
        sh_ready = sem("sh_ready")
        sl_ready = sem("sl_ready")
        tr_p = sem("tr_p")
        tr_d = sem("tr_d")
        hi_ready = sem("hi_ready")
        lo_p = sem("lo_p")
        lo_d = sem("lo_d")
        multiplied = sem("multiplied")
        folded = sem("folded")
        summed_tile = sem("summed_tile")
        summed_d = sem("summed_d")
        parts_read = sem("parts_read")
        across_done = sem("across_done")
        deg_ready = sem("deg_ready")
        sqrt_ready = sem("sqrt_ready")
        dinv_ready = sem("dinv_ready")
        head_out = sem("head_out")
        tail_out = sem("tail_out")
        y_ready = sem("y_ready")
        rows_loaded = sem("rows_loaded")
        mv_ready = sem("mv_ready")
        var_ready = sem("var_ready")
        std_ready = sem("std_ready")
        rstd_ready = sem("rstd_ready")
        x1_ready = sem("x1_ready")
        x1_trans = sem("x1_trans")
        x1t_ready = sem("x1t_ready")
        p_ready = sem("p_ready")
        u_ready = sem("u_ready")
        u_stored = sem("u_stored")
        uh_ready = sem("uh_ready")
        ul_ready = sem("ul_ready")
        bias_added = sem("bias_added")
        rows_done = sem("rows_done")
        rows_stored = sem("rows_stored")
        chain = sem("chain")

        block = ctx.enter_context(nc.Block())

        def wait_chunk_loaded(eng, g, ps, c):
            i = c % SLOTS
            before = sum(per_slot(k) for k, _, _ in PASSES[ps][1][i:c:SLOTS])
            eng.wait_ge(loaded[i], base(g, [n[i] for n in SLOT_INC], ps) + before + per_slot(PASSES[ps][1][c][0]))

        def wait_chunk_free(eng, g, ps, c):
            kind, n, _ = PASSES[ps][1][c]
            if kind == "P":
                gone = base(g, NPT, ps) + (n + 1) * SPC * PAIR
                eng.wait_ge(tr_p, gone)
                if ps == 0:
                    eng.wait_ge(summed_tile, gone)
            elif ps == 0:
                eng.wait_ge(summed_d, base(g, DCH, ps) + n + 1)
            else:
                eng.wait_ge(tr_d, base(g, ND, ps) + (n + 1) * SPC)

        def load_d(eng, row_block, ps, c, quadrants):
            i, n = c % SLOTS, PASSES[ps][1][c][1]
            for q in quadrants:
                col = q * DQ[ps] + n * QCOLS
                eng.dma_start(chunk[q * Q:(q + 1) * Q, i, :].rearrange("c (b k) -> c b k", k=QCOLS),
                              adj_d[row_block, :, :, col:col + QCOLS]).then_inc(loaded[i], 16)

        SP_QUADRANTS, ACT_QUADRANTS = (0, 1), (2, 3)

        def d_view(slot):
            return chunk[:, slot, :].rearrange("p (b k) -> p b k", k=QCOLS)

        def p_view(slot):
            return chunk[:, slot, :].rearrange("p (r k) -> p r k", k=CCOLS)

        def part_view(part):
            return chunk[:, SLOTS - PARTS + part, :].rearrange("p (t f) -> p t f", f=F)

        def part_tiles(ps, part):
            return XT - R if ps == 1 and part == PARTS - 1 else XT

        def part_pieces(ps, part):
            lo, hi = part * XT, part * XT + part_tiles(ps, part)
            edge = min(max(PAIR * ND[ps], lo), hi)
            pieces = [(q, lo, edge - lo) for q in range(QN)] if edge > lo else []
            return pieces + ([(None, edge, hi - edge)] if hi > edge else [])

        def staged_count(ps, part):
            return 16 * (len(part_pieces(0, part)) + (len(part_pieces(1, part)) if ps else 0))

        @block.sync
        def _(sp):
            def stage(ps, part, source):
                for q, tile, n in part_pieces(ps, part):
                    at = tile - part * XT
                    if q is None:
                        row = DCOLS[ps] + (tile - PAIR * ND[ps]) * P
                        sp.dma_start(part_view(part)[:, at:at + n, :],
                                     source[row:row + n * P, :].rearrange("(t p) f -> p t f", p=P)
                                     ).then_inc(staged[part], 16)
                    else:
                        row = q * DQ[ps] + tile * Q
                        sp.dma_start(part_view(part)[q * Q:(q + 1) * Q, at:at + n, :],
                                     source[row:row + n * Q, :].rearrange("(t a) f -> a t f", a=Q)
                                     ).then_inc(staged[part], 16)

            def load_chunk(g, row_block, ps, c):
                kind, n, _ = PASSES[ps][1][c]
                if kind == "D":
                    load_d(sp, row_block, ps, c, SP_QUADRANTS)
                else:
                    col = DCOLS[ps] + n * CCOLS
                    sp.dma_start(p_view(c % SLOTS), adj_p[row_block, :, :, col:col + CCOLS]
                                 ).then_inc(loaded[c % SLOTS], 16)

            def load_rows(row_block, second):
                if second:
                    sp.dma_start(rows[:, :, :], resid[row_block]).then_inc(rows_loaded, 16)
                else:
                    sp.dma_start(rows[:, :, :], h_v[row_block]).then_inc(rows_loaded, 16)
                    sp.dma_start(rows2[:, :, :], x_v[row_block]).then_inc(rows_loaded, 16)

            def store_rows(g, row_block, second):
                sp.wait_ge(rows_done, 16 * g)
                sp.dma_start((out_v if second else resid)[row_block], rows[:, :, :]).then_inc(rows_stored, 16)

            def store_u(g, row_block):
                sp.wait_ge(u_ready, 16 * g)
                sp.dma_start(u_v[row_block], rows2[:, :, :]).then_inc(u_stored, 16)

            def run_block(g, ps, row_work):
                opening = isinstance(g, int) and g in (0, BLOCKS)
                row_block = g - BLOCKS * ps
                done = g - 1 if row_work != "second" else g - 1 - BLOCKS
                for c in range(CHUNKS):
                    if opening and c == SLOTS - PARTS:
                        for part in PART_ORDER:
                            if ps == 1:
                                wait_chunk_free(sp, g - 1, 0, CHUNKS - PARTS + part)
                                sp.wait_ge(u_stored, 16 * (BLOCKS - 1))
                            stage(ps, part, x if ps == 0 else u_dram)
                    if c >= SLOTS:
                        wait_chunk_free(sp, g, ps, c - SLOTS)
                    elif opening and c >= SLOTS - PARTS:
                        sp.wait_ge(sl_ready, PARTS * ps + PART_ORDER.index(c - SLOTS + PARTS) + 1)
                    elif not (isinstance(g, int) and g == 0):
                        wait_chunk_free(sp, g - 1, 0 if opening else ps, c + SLOTS)
                    if row_work and c == CHUNKS - 1:
                        sp.wait_ge(rows_stored, 16 * g)
                        if row_work == "first":
                            sp.wait_ge(u_stored, 16 * g)
                    load_chunk(g, row_block, ps, c)
                    if row_work and c == 5:
                        load_rows(done, row_work == "second")
                    if row_work and c == CHUNKS - 3:
                        store_rows(g, done, row_work == "second")
                        if row_work == "first":
                            store_u(g, done)

            sp.dma_start(feat[:, 0:F], W[:, :]).then_inc(w_loaded, 16)
            sp.dma_start(b_bc[:, :], b.rearrange("(o f) -> o f", o=1).broadcast_to([P, F])).then_inc(b_loaded, 16)
            run_block(0, 0, None)
            with sp.Fori(1, BLOCKS) as g:
                run_block(g, 0, "first")
            run_block(BLOCKS, 1, "last of first")
            with sp.Fori(BLOCKS + 1, ALL) as g:
                run_block(g, 1, "second")
            load_rows(BLOCKS - 1, True)
            store_rows(ALL, BLOCKS - 1, True)
            sp.wait_ge(rows_stored, 16 * ALL)

        @block.gpsimd
        def _(pool):
            nc.gpsimd.memset(ident[:, :], 0.0).then_inc(zeroed, 1)
            nc.gpsimd.memset(spread[:, :], 0.0).then_inc(zeroed, 1)
            pool.wait_ge(zeroed, 2)
            nc.gpsimd.affine_select(out=ident[:, :], in_=ident[:, :], compare_op=ALU.not_equal, fill=1.0,
                                    base=0, pattern=[[-1, P]], channel_multiplier=1).then_inc(consts_ready, 1)
            middle = spread[:, (QN - 1) * Q:QN * Q]
            for q in range(QN):
                ins = nc.gpsimd.affine_select(out=middle, in_=middle, compare_op=ALU.not_equal, fill=1.0,
                                              base=-q * Q, pattern=[[-1, Q]], channel_multiplier=1)
                ins.then_inc(zeroed, 1)
                pool.wait_ge(zeroed, 3 + q)
                if q == QN - 1:
                    nc.gpsimd.memset(unused[:, 0:1], 0.0).then_inc(consts_ready, 1)

            def make_lo(g, s, entry, ps):
                _, n, _, _ = entry
                pool.wait_ge(hi_ready, g * STEPS + s + 1)
                if not in_first(g, s - LOS):
                    pool.wait_ge(multiplied, g * STEPS + s - LOS + 1)
                nc.gpsimd.tensor_tensor(a_lo[:, s % LOS, :], a_tr[:, n % TRS, :],
                                        a_hi[:, s % HIS, :].bitcast(fp32), ALU.subtract).then_inc(lo_d, 1)

            def fold_chunk(g, n, c):
                wait_chunk_loaded(pool, g, 0, c)
                if not in_first(g, n - 2):
                    pool.wait_ge(summed_d, base(g, DCH, 0) + n - 1)
                v = d_view(c % SLOTS)
                nc.gpsimd.tensor_tensor(fold[:, :, :], v[:, :, 0:FOLD], v[:, :, FOLD:QCOLS],
                                        ALU.add).then_inc(folded, 1)

            def run_slot(g, t, ps):
                todo = ahead(g, t, LEAD_LO, ps)
                if todo and todo[2][0] == "D":
                    make_lo(*todo, ps)
                if ps == 0 and t >= 0 and t % 8 == 0:
                    fold_chunk(g, t // 4, t // 2)

            def run_block(g, ps):
                for t in range(STEPS):
                    run_slot(g, t, ps)

            for t in range(-LEAD_LO, 0):
                run_slot(0, t, 0)
            run_block(0, 0)
            with pool.Fori(1, BLOCKS) as g:
                run_block(g, 0)
            with pool.Fori(BLOCKS, ALL - 1) as g:
                run_block(g, 1)
            run_block(ALL - 1, 1)

        @block.tensor
        def _(pe):
            def transpose_step(g, s, entry, ps):
                _, n, c, place = entry
                if place == 0:
                    wait_chunk_loaded(pe, g, ps, c)
                if not in_first(g, n - 2):
                    pe.wait_ge(lo_p, base(g, NP, ps) + n - 1)
                for t in range(PAIR):
                    col = (place * PAIR + t) * P
                    for r in range(R):
                        last = nc.tensor.transpose(a_ps[n % 2][:, (t * R + r) * P:(t * R + r + 1) * P],
                                                   p_view(c % SLOTS)[:, r, col:col + P], ident[:, :])
                last.then_inc(tr_p, PAIR)

            def multiply_step(g, s, ps):
                kind, n, _, _ = PASSES[ps][0][s]
                acc = acc_head if s < HEAD else acc_tail
                first, final = s in (0, HEAD), s in (HEAD - 1, STEPS - 1)
                tile = stationary(ps, s)
                pe.wait_ge(hi_ready, g * STEPS + s + 1)
                for t in range(PAIR):
                    moving = a_hi[:, s % HIS, t * ROWS:(t + 1) * ROWS]
                    nc.tensor.matmul(acc[:, :], s_hi[:, tile + t, :], moving, start=first and t == 0, stop=False)
                    nc.tensor.matmul(acc[:, :], s_lo[:, tile + t, :], moving, start=False, stop=False)
                todo = ahead(g, s, LEAD_P, ps)
                if todo and todo[2][0] == "P":
                    transpose_step(*todo, ps)
                if kind == "D":
                    pe.wait_ge(lo_d, base(g, ND, ps) + n + 1)
                else:
                    pe.wait_ge(lo_p, base(g, NP, ps) + n + 1)
                for t in range(PAIR):
                    last = nc.tensor.matmul(acc[:, :], s_hi[:, tile + t, :],
                                            a_lo[:, s % LOS, t * ROWS:(t + 1) * ROWS],
                                            start=False, stop=final and t == PAIR - 1)
                last.then_inc(multiplied, 1)

            def row_sums_across(g):
                pe.wait_ge(parts_read, g)
                for v in range(QN):
                    last = nc.tensor.matmul(x1_ps[:, 0:R], spread[:, (QN - 1 - v) * Q:(2 * QN - 1 - v) * Q],
                                            sum_d[:, v:RB:QN], start=v == 0, stop=v == QN - 1)
                last.then_inc(across_done, 1)

            def rows_back(g):
                pe.wait_ge(tail_out, g)
                for r in range(R):
                    last = nc.tensor.transpose(row_ps[:, r * P:(r + 1) * P], feat[:, r * P:(r + 1) * P], ident[:, :])
                last.then_inc(y_ready, 1)

            def x1_transpose(g):
                pe.wait_ge(x1_ready, g)
                for r in range(R):
                    last = nc.tensor.transpose(x1_ps[:, r * P:(r + 1) * P], rows[:, r, :], ident[:, :])
                last.then_inc(x1_trans, 1)

            def x1_weights(g):
                pe.wait_ge(x1t_ready, g)
                for r in range(R):
                    last = nc.tensor.matmul(row_ps[:, r * P:(r + 1) * P], feat[:, r * P:(r + 1) * P], w_t[:, :],
                                            start=True, stop=True)
                last.then_inc(p_ready, 1)

            def run_block(g, ps, row_work):
                opening = isinstance(g, int) and g in (0, BLOCKS)
                seen = 0
                for s in range(STEPS):
                    if opening:
                        need = PART_ORDER.index(stationary(ps, s) // XT) + 1
                        if need > seen:
                            pe.wait_ge(sl_ready, PARTS * ps + need)
                            seen = need
                    if opening and ps == 1 and s == STEPS - SPC:
                        pe.wait_ge(ul_ready, 1)
                    if row_work and s == 0:
                        pe.wait_ge(head_out, g)
                    if row_work and s == HEAD:
                        pe.wait_ge(tail_out, g)
                    multiply_step(g, s, ps)
                    if row_work and row_work != "second" and s == 2:
                        row_sums_across(g)
                    if row_work and s == 4:
                        rows_back(g)
                    if row_work and row_work != "second" and s == 13:
                        x1_transpose(g)
                    if row_work and row_work != "second" and s == 16:
                        x1_weights(g)

            pe.wait_ge(consts_ready, 2)
            pe.wait_ge(w_loaded, 16)
            nc.tensor.transpose(row_ps[:, 0:F], feat[:, 0:F], ident[:, :]).then_inc(w_trans, 1)
            for t in range(-LEAD_P, 0):
                todo = ahead(0, t, LEAD_P, 0)
                if todo[2][0] == "P":
                    transpose_step(*todo, 0)
            pe.wait_ge(w_ready, 1)
            run_block(0, 0, None)
            with pe.Fori(1, BLOCKS) as g:
                run_block(g, 0, "first")
            run_block(BLOCKS, 1, "last of first")
            with pe.Fori(BLOCKS + 1, ALL - 1) as g:
                run_block(g, 1, "second")
            run_block(ALL - 1, 1, "second")
            rows_back(ALL)

        @block.scalar
        def _(act):
            def make_hi(g, s, entry, ps):
                kind, n, _, _ = entry
                if kind == "D":
                    act.wait_ge(tr_d, base(g, ND, ps) + n + 1)
                    source = a_tr[:, n % TRS, :]
                else:
                    act.wait_ge(tr_p, base(g, NPT, ps) + (n + 1) * PAIR)
                    source = a_ps[n % 2][:, :]
                if not in_first(g, s - HIS):
                    act.wait_ge(multiplied, g * STEPS + s - HIS + 1)
                nc.scalar.activation(a_hi[:, s % HIS, :], source, ACT.Copy).then_inc(hi_ready, 1)

            def sum_chunk(g, n, c, tiles):
                if tiles[0] == 0:
                    wait_chunk_loaded(act, g, 0, c)
                    if n == 0 and not in_first(g, -1):
                        act.wait_ge(parts_read, g)
                for r in tiles:
                    if not in_first(g, n * R + r - 1):
                        act.wait_ge(summed_tile, (g * PCH[0] + n) * R + r)
                    nc.scalar.activation(unused[:, :], p_view(c % SLOTS)[:, r, :], ACT.Copy,
                                         accum_out=part_p[:, r, n:n + 1]).then_inc(summed_tile, 1)

            def root_degrees(g):
                act.wait_ge(deg_ready, g)
                nc.scalar.activation(sqrt_deg[:, :], deg[:, :], ACT.Sqrt).then_inc(sqrt_ready, 1)

            def deviation(g):
                act.wait_ge(var_ready, g)
                nc.scalar.activation(std[:, :], std[:, :], ACT.Sqrt).then_inc(std_ready, 1)

            def x1_copy(g):
                act.wait_ge(x1_trans, g)
                nc.scalar.activation(feat[:, :], x1_ps[:, :], ACT.Copy).then_inc(x1t_ready, 1)

            def make_u(g, last_block):
                act.wait_ge(p_ready, g)
                act.wait_ge(dinv_ready, g)
                for r in range(R):
                    to = s_hi[:, JT - R + r, :] if last_block else rows2[:, r, :]
                    last = nc.scalar.activation(to, row_ps[:, r * P:(r + 1) * P], ACT.Copy, scale=dinv[:, r:r + 1])
                if last_block:
                    last.then_inc(uh_ready, 1)
                else:
                    last.then_inc(u_ready, 16)

            def take_head(g, row_work):
                if row_work == "second":
                    act.wait_ge(y_ready, g)
                elif row_work:
                    act.wait_ge(p_ready, g)
                act.wait_ge(multiplied, g * STEPS + HEAD)
                nc.scalar.activation(feat[:, :], acc_head[:, :], ACT.Copy).then_inc(head_out, 1)

            def split_part(ps, i):
                part = PART_ORDER[i]
                n = part_tiles(ps, part)
                act.wait_ge(staged[part], staged_count(ps, part))
                if ps == 1 and i == 0:
                    act.wait_ge(multiplied, BLOCKS * STEPS)
                nc.scalar.activation(s_hi[:, part * XT:part * XT + n, :], part_view(part)[:, 0:n, :],
                                     ACT.Copy).then_inc(sh_ready, 1)

            def load_slot(g, t, ps, ps_next):
                for c in range(CHUNKS):
                    if min(PASSES[ps][1][c][2] + 1, STEPS - 1) != t:
                        continue
                    if c < SLOTS and PASSES[ps][1][c + SLOTS][0] == "D":
                        wait_chunk_free(act, g, ps, c)
                        load_d(act, g - BLOCKS * ps, ps, c + SLOTS, ACT_QUADRANTS)
                    n = c - SLOTS
                    if n < 0 or ps_next is None or PASSES[ps_next][1][n][0] != "D":
                        continue
                    if ps_next != ps and n >= SLOTS - PARTS:
                        continue
                    wait_chunk_free(act, g, ps, c)
                    load_d(act, g + 1 - BLOCKS * ps_next, ps_next, n, ACT_QUADRANTS)

            def load_after_split(ps, i):
                c = SLOTS - PARTS + PART_ORDER[i]
                if PASSES[ps][1][c][0] == "D":
                    act.wait_ge(sl_ready, PARTS * ps + i + 1)
                    load_d(act, 0, ps, c, ACT_QUADRANTS)

            def run_slot(g, t, ps):
                todo = ahead(g, t, LEAD_HI, ps)
                if todo:
                    make_hi(*todo, ps)

            def run_block(g, ps, row_work, ps_next):
                opening = isinstance(g, int) and g in (0, BLOCKS)
                for t in range(STEPS):
                    run_slot(g, t, ps)
                    if opening and t in (1, 3):
                        split_part(ps, 2 + t // 2)
                        load_after_split(ps, t // 2)
                    if opening and t in (5, 7):
                        load_after_split(ps, 2 + (t - 5) // 2)
                    if ps == 0:
                        n, k = t // 4, t % 4
                        if n > 0:
                            sum_chunk(g, n, 2 * n + 1, (k,))
                        elif k >= 2:
                            sum_chunk(g, 0, 1, (2 * k - 4, 2 * k - 3))
                    if row_work and row_work != "second":
                        if t == 6:
                            root_degrees(g)
                        if t == 15:
                            x1_copy(g)
                        if t == 18:
                            make_u(g, row_work == "last of first")
                    if row_work and t == 10:
                        deviation(g)
                    if t == 22:
                        take_head(g, row_work)
                    load_slot(g, t, ps, ps_next)

            for c in range(SLOTS - PARTS):
                if PASSES[0][1][c][0] == "D":
                    load_d(act, 0, 0, c, ACT_QUADRANTS)
            act.wait_ge(w_trans, 1)
            nc.scalar.activation(w_t[:, :], row_ps[:, 0:F], ACT.Copy).then_inc(w_ready, 1)
            split_part(0, 0)
            split_part(0, 1)
            for t in range(-LEAD_HI, 0):
                run_slot(0, t, 0)
            run_block(0, 0, None, 0)
            with act.Fori(1, BLOCKS - 1) as g:
                run_block(g, 0, "first", 0)
            run_block(BLOCKS - 1, 0, "first", 1)
            split_part(1, 0)
            split_part(1, 1)
            run_block(BLOCKS, 1, "last of first", 1)
            with act.Fori(BLOCKS + 1, ALL - 1) as g:
                run_block(g, 1, "second", 1)
            run_block(ALL - 1, 1, "second", None)
            deviation(ALL)

        @block.vector
        def _(dve):
            CHAIN = (5, 3)

            def link(ins):
                return ins.then_inc(chain, 1)

            def transpose_step(g, s, entry, ps):
                _, n, c, place = entry
                if place == 0:
                    wait_chunk_loaded(dve, g, ps, c)
                if not in_first(g, n - TRS):
                    dve.wait_ge(lo_d, used_before(g, n, TRS, ND, ps))
                for t in range(PAIR):
                    col = (place * PAIR + t) * Q
                    last = nc.vector.transpose(a_tr[:, n % TRS, t * ROWS:(t + 1) * ROWS],
                                               d_view(c % SLOTS)[:, :, col:col + Q])
                last.then_inc(tr_d, 1)

            def make_lo(g, s, entry, ps):
                _, n, _, _ = entry
                dve.wait_ge(hi_ready, g * STEPS + s + 1)
                if not in_first(g, s - LOS):
                    dve.wait_ge(multiplied, g * STEPS + s - LOS + 1)
                nc.vector.tensor_tensor(a_lo[:, s % LOS, :], a_ps[n % 2][:, :],
                                        a_hi[:, s % HIS, :].bitcast(fp32), ALU.subtract).then_inc(lo_p, 1)

            def sum_chunk(g, n, c, half):
                b = slice(half * HALF, (half + 1) * HALF)
                if n == 0 and half == 0 and not in_first(g, -1):
                    dve.wait_ge(parts_read, g)
                if n % 2 == 0:
                    dve.wait_ge(folded, g * (DCH[0] // 2) + n // 2 + 1)
                    source = fold[:, b, :]
                else:
                    source = d_view(c % SLOTS)[:, b, :]
                last = nc.vector.tensor_reduce(part_d[:, b, n:n + 1], source, AX.X, ALU.add)
                if half == 1:
                    last.then_inc(summed_d, 1)

            def sum_parts(g, at):
                dve.wait_ge(summed_tile, g * PCH[0] * R)
                dve.wait_ge(summed_d, base(g, DCH, 0))
                link(nc.vector.tensor_reduce(sum_p[:, :], part_p[:, :, :], AX.X, ALU.add))
                nc.vector.tensor_reduce(sum_d[:, :], part_d[:, :, :], AX.X, ALU.add).then_inc(parts_read, 1)

            def degrees(g, at):
                dve.wait_ge(chain, at + 1)
                dve.wait_ge(across_done, g)
                link(nc.vector.tensor_tensor(deg[:, :], x1_ps[:, 0:R], sum_p[:, :], ALU.add))
                dve.wait_ge(chain, at + 2)
                nc.vector.tensor_scalar(deg[:, :], deg[:, :], 1.0, None, ALU.add).then_inc(deg_ready, 1)

            def inverse_degrees(g, row_block):
                dve.wait_ge(sqrt_ready, g)
                nc.vector.reciprocal(dinv[:, :], sqrt_deg[:, :])
                nc.vector.reciprocal(dinv_all[:, bass.ds(row_block * R, R)], sqrt_deg[:, :])
                nc.vector.reciprocal(dinv2[:, :], deg[:, :]).then_inc(dinv_ready, 1)

            def take_dinv(row_block, at):
                link(nc.vector.tensor_copy(dinv[:, :], dinv_all[:, bass.ds(row_block * R, R)]))

            def add_tail(g):
                dve.wait_ge(multiplied, g * STEPS)
                dve.wait_ge(head_out, g)
                nc.vector.tensor_tensor(feat[:, :], acc_tail[:, :], feat[:, :], ALU.add).then_inc(tail_out, 1)

            def mix_inputs(g, at):
                dve.wait_ge(rows_loaded, 32 * g)
                link(nc.vector.scalar_tensor_tensor(rows[:, :, :], rows[:, :, :], ALPHA, rows2[:, :, :],
                                                    ALU.mult, ALU.add))

            def first_rows(g, at):
                dve.wait_ge(y_ready, g)
                dve.wait_ge(chain, at + 3)
                link(nc.vector.scalar_tensor_tensor(rows[:, :, :], row_ps[:, :].rearrange("p (r f) -> p r f", f=F),
                                                    1.0 - ALPHA, rows[:, :, :], ALU.mult, ALU.add))

            def second_rows(g, at):
                dve.wait_ge(chain, at + 1)
                dve.wait_ge(y_ready, g)
                dve.wait_ge(rows_loaded, 16 * g + 16 * BLOCKS)
                for r in range(R):
                    last = nc.vector.scalar_tensor_tensor(rows[:, r, :], row_ps[:, r * P:(r + 1) * P],
                                                          dinv[:, r:r + 1], rows[:, r, :], ALU.mult, ALU.add)
                link(last)

            def statistics(seen):
                dve.wait_ge(chain, seen)
                for r in range(R):
                    last = nc.vector.bn_stats(stats[:, r, :], rows[:, r, :])
                link(last)

            def variance(seen):
                dve.wait_ge(chain, seen)
                nc.vector.memset(carrier[:, :], 0.0)
                for r in range(R):
                    last = nc.vector.bn_aggr(mv[:, r, :], stats[:, r, :])
                last.then_inc(mv_ready, 1)

            def add_eps(g):
                dve.wait_ge(mv_ready, g)
                nc.vector.tensor_scalar(std[:, :], mv[:, :, 1], EPS, None, ALU.add).then_inc(var_ready, 1)

            def inverse_deviation(g):
                dve.wait_ge(std_ready, g)
                nc.vector.reciprocal(rstd[:, :], std[:, :]).then_inc(rstd_ready, 1)

            def normalise(g, done, by):
                dve.wait_ge(rstd_ready, g)
                for r in range(R):
                    last = nc.vector.tensor_scalar(rows[:, r, :], rows[:, r, :], mv[:, r, 0:1], rstd[:, r:r + 1],
                                                   ALU.subtract, ALU.mult)
                last.then_inc(done, by)

            def last_u_low(g):
                dve.wait_ge(uh_ready, 1)
                for r in range(R):
                    last = nc.vector.scalar_tensor_tensor(s_lo[:, JT - R + r, :], row_ps[:, r * P:(r + 1) * P],
                                                          dinv[:, r:r + 1], s_hi[:, JT - R + r, :].bitcast(fp32),
                                                          ALU.mult, ALU.subtract)
                last.then_inc(ul_ready, 1)

            def residual_bias(g):
                dve.wait_ge(x1_trans, g)
                bias = b_bc[:, :].rearrange("p (o f) -> p o f", o=1).broadcast_to([P, R, F])
                nc.vector.tensor_tensor(rows[:, :, :], rows[:, :, :], bias, ALU.add).then_inc(bias_added, 1)

            def residual(g, last_block):
                dve.wait_ge(bias_added, g)
                if last_block:
                    dve.wait_ge(uh_ready, 1)
                else:
                    dve.wait_ge(u_ready, 16 * g)
                for r in range(R):
                    last = nc.vector.scalar_tensor_tensor(rows[:, r, :], row_ps[:, r * P:(r + 1) * P],
                                                          dinv2[:, r:r + 1], rows[:, r, :], ALU.mult, ALU.add)
                last.then_inc(rows_done, 16)

            def split_part(ps, i):
                part = PART_ORDER[i]
                n = part_tiles(ps, part)
                dve.wait_ge(sh_ready, PARTS * ps + i + 1)
                nc.vector.tensor_tensor(s_lo[:, part * XT:part * XT + n, :], part_view(part)[:, 0:n, :],
                                        s_hi[:, part * XT:part * XT + n, :].bitcast(fp32),
                                        ALU.subtract).then_inc(sl_ready, 1)

            def run_slot(g, t, ps):
                todo = ahead(g, t, LEAD_D, ps)
                if todo and todo[2][0] == "D":
                    transpose_step(*todo, ps)
                todo = ahead(g, t, LEAD_LO, ps)
                if todo and todo[2][0] == "P":
                    make_lo(*todo, ps)

            def first_row_work(g, t, at, last_block):
                if t == 0:
                    sum_parts(g, at)
                if t == 1:
                    add_tail(g)
                if t == 4:
                    degrees(g, at)
                if t == 6:
                    mix_inputs(g, at)
                if t == 7:
                    first_rows(g, at)
                if t == 8:
                    inverse_degrees(g, g - 1)
                    statistics(at + 4)
                if t == 9:
                    variance(at + 5)
                    add_eps(g)
                if t == 11:
                    inverse_deviation(g)
                if t == 12:
                    normalise(g, x1_ready, 1)
                if t == 16:
                    residual_bias(g)
                if t == 19 and last_block:
                    last_u_low(g)
                if t == 19:
                    residual(g, last_block)

            def second_row_work(g, t, at):
                if t == 1:
                    add_tail(g)
                if t == 3:
                    take_dinv(g - 1 - BLOCKS, at)
                if t == 7:
                    second_rows(g, at)
                if t == 8:
                    statistics(at + 2)
                if t == 9:
                    variance(at + 3)
                    add_eps(g)
                if t == 11:
                    inverse_deviation(g)
                if t == 12:
                    normalise(g, rows_done, 16)

            def run_block(g, ps, row_work):
                opening = isinstance(g, int) and g in (0, BLOCKS)
                for t in range(STEPS):
                    run_slot(g, t, ps)
                    if opening and t in (1, 3):
                        split_part(ps, 2 + t // 2)
                    if row_work in ("first", "last of first"):
                        first_row_work(g, t, (g - 1) * CHAIN[0], row_work == "last of first")
                    if row_work == "second":
                        second_row_work(g, t, BLOCKS * CHAIN[0] + (g - 1 - BLOCKS) * CHAIN[1])
                    if ps == 0:
                        n, k = t // 4, t % 4
                        if n % 2 == 0 and k >= 2:
                            sum_chunk(g, n, 2 * n, k - 2)
                        if n % 2 == 1 and k < 2:
                            sum_chunk(g, n, 2 * n, k)

            split_part(0, 0)
            split_part(0, 1)
            dve.wait_ge(b_loaded, 16)
            for t in range(-LEAD_D, 0):
                run_slot(0, t, 0)
            run_block(0, 0, None)
            with dve.Fori(1, BLOCKS) as g:
                run_block(g, 0, "first")
            split_part(1, 0)
            split_part(1, 1)
            run_block(BLOCKS, 1, "last of first")
            with dve.Fori(BLOCKS + 1, ALL - 1) as g:
                run_block(g, 1, "second")
            run_block(ALL - 1, 1, "second")
            for t in range(STEPS):
                second_row_work(ALL, t, BLOCKS * CHAIN[0] + (ALL - 1 - BLOCKS) * CHAIN[1])


_INS = ["x", "adj", "L0_gnn_h", "L1_gnn_W", "L1_gnn_b"]


def kernel(**inputs):
    import numpy as _np
    import concourse.bacc as _bacc
    from concourse import mybir as _mybir
    from concourse.bass_utils import run_bass_kernel_spmd as _run

    nc = _bacc.Bacc("TRN2", target_bir_lowering=False, num_devices=1)
    arrays, args = {}, []
    for name in _INS:
        a = _np.ascontiguousarray(inputs[name])
        arrays[f"in_{name}_dram"] = a
        args.append(nc.dram_tensor(f"in_{name}_dram", a.shape, _mybir.dt.from_np(a.dtype), kind="ExternalInput").ap())
    shape = tuple(inputs["x"].shape)
    args.append(nc.dram_tensor("out_dram", shape, _mybir.dt.float32, kind="ExternalOutput").ap())
    graph_resnorm_kernel(nc, *args)
    r = _run(nc, [arrays], core_ids=[0])
    return r.results[0]["out_dram"]
```

```python
import concourse.bass as bass
from concourse import mybir
from contextlib import ExitStack



class Step:

    def __init__(self, kind, before, chunk, place):
        self.kind = kind
        self.chunk, self.place = chunk, place
        self.blocky = sum(k != "P" for k in before)
        self.d = sum(k == "D" for k in before)
        self.p = sum(k == "P" for k in before)
        self.ps = sum(k != "D" for k in before)


def plan(kinds):
    steps, chunks, opened = [], [], {}
    for s, kind in enumerate(kinds):
        sort = "P" if kind == "P" else "D"
        n = sum((k == "P") == (kind == "P") for k in kinds[:s])
        if n % 2 == 0:
            opened[sort] = len(chunks)
            chunks.append(None)
        chunks[opened[sort]] = (sort, n // 2, s)
        steps.append(Step(kind, kinds[:s], opened[sort], n % 2))
    return steps, chunks


FIRST_PASS = plan("DP" * 16)
SECOND_PASS = plan("DPDPDDVDDPDDVDPDDDVDPDDDVDPDDDPP")


def graph_resnorm_kernel(nc, x, adj, h, W, b, out):
    fp32 = mybir.dt.float32
    f32r = mybir.dt.float32r
    bf16 = mybir.dt.bfloat16
    ALU = mybir.AluOpType
    ACT = mybir.ActivationFunctionType
    AX = mybir.AxisListType

    N, F = x.shape
    P = 128
    Q = 32
    QN = P // Q
    ALPHA = 0.1
    EPS = 1e-5
    ROWS = 512
    R = ROWS // P
    RB = ROWS // Q
    BLOCKS = N // ROWS
    PAIR = 2
    JT = N // P
    STEPS = JT // PAIR
    SPC = 2
    CCOLS = SPC * PAIR * P
    QCOLS = CCOLS // QN
    CHUNKS = N // CCOLS
    SLOTS = 8
    HIS, LOS, TRS = 8, 4, 4
    HEAD = 4
    LEAD_D, LEAD_P, LEAD_HI, LEAD_LO = 5, 4, 3, 2
    PARTS = 4
    XT = JT // PARTS
    CONTENT = ((("D", 0), ("D", XT), ("P", 0), ("P", XT)), (("P", 0), ("D", XT), ("D", 0), ("D", 2 * XT)))
    STAGE_CHUNK = ((5, 9, 7, 11), (3, 8, 2, 10))
    PART_ORDER = ((0, 2, 1, 3), (2, 0, 1, 3))
    STAGE_BEFORE = ((1, 2, 9, 9), (1, 1, 6, 8))
    SPLIT_LAST = ((10, 12), (5, 9))
    U_LAST = XT - R
    FOLDED = (0, 1, 2, 4, 5, 6)
    SPLIT_U = (26, 29)
    ALL = 2 * BLOCKS
    PASSES = (FIRST_PASS, SECOND_PASS)
    NBLOCKY = [sum(s.kind != "P" for s in p[0]) for p in PASSES]
    ND = [sum(s.kind == "D" for s in p[0]) for p in PASSES]
    NPS = [STEPS - n for n in ND]
    NPT = [PAIR * (STEPS - n) for n in NBLOCKY]
    DCH = [n // SPC for n in NBLOCKY]
    PCH = [n // SPC // PAIR for n in NPT]
    DQ = [n * QCOLS for n in DCH]
    DCOLS = [QN * n for n in DQ]
    FOLD = QCOLS // 2
    HALF = RB // 2

    adj_p = adj.rearrange("(n r p) m -> n p r m", r=R, p=P)
    adj_d = adj.rearrange("(n b c) m -> n c b m", b=RB, c=Q)
    x_v = x.rearrange("(n r p) f -> n p r f", r=R, p=P)
    h_v = h.rearrange("(n r p) f -> n p r f", r=R, p=P)
    out_v = out.rearrange("(n r p) f -> n p r f", r=R, p=P)
    resid = nc.dram_tensor("resid", (BLOCKS, P, R, F), fp32, kind="Internal").ap()
    u_dram = nc.dram_tensor("u_dram", (N, F), fp32, kind="Internal").ap()
    u_v = u_dram.rearrange("(n r p) f -> n p r f", r=R, p=P)

    def per_slot(k):
        return 16 * QN if k == "D" else 16

    SLOT_INC = [[sum(per_slot(c[0]) for c in p[1][i::SLOTS]) for i in range(SLOTS)] for p in PASSES]

    def base(g, counts, ps):
        if ps == 0:
            return g * counts[0]
        return g * counts[1] + BLOCKS * (counts[0] - counts[1])

    def stationary(ps, s):
        step = PASSES[ps][0][s]
        kind, n = ("P", PAIR * step.p) if step.kind == "P" else ("D", PAIR * step.blocky)
        return CONTENT[ps].index((kind, n // XT * XT)) * XT + n % XT

    def ahead(g, t, lead, ps):
        u = t + lead
        if u < 0 or isinstance(g, int) and g * STEPS + u >= ALL * STEPS:
            return None
        if u >= STEPS:
            return g + 1, u - STEPS, PASSES[ps][0][u - STEPS]
        return g, u, PASSES[ps][0][u]

    def used_before(g, n, ring, counts, ps):
        if n >= ring:
            return base(g, counts, ps) + n - ring + 1
        before = counts[0 if isinstance(g, int) and g == BLOCKS else ps]
        last = max(m for m in range(before) if m % ring == n)
        return base(g, counts, ps) - before + last + 1

    def in_first(g, n):
        return isinstance(g, int) and g == 0 and n < 0

    ctx = ExitStack()
    with ctx:
        def sb(name, shape, dt=fp32):
            return ctx.enter_context(nc.sbuf_tensor(name, shape, dt))

        def pb(name, shape, dt=fp32):
            return ctx.enter_context(nc.psum_tensor(name, shape, dt))

        def sem(name):
            return ctx.enter_context(nc.semaphore(name))

        s_hi = sb("s_hi", [P, JT, F], f32r)
        s_lo = sb("s_lo", [P, JT, F], f32r)
        chunk = sb("chunk", [P, SLOTS, R * CCOLS])
        a_tr = sb("a_tr", [P, TRS, PAIR * ROWS])
        a_hi = sb("a_hi", [P, HIS, PAIR * ROWS], f32r)
        a_lo = sb("a_lo", [P, LOS, PAIR * ROWS], f32r)
        fold = sb("fold", [P, RB, FOLD])
        feat = sb("feat", [P, ROWS])
        rows = sb("rows", [P, R, F])
        rows2 = sb("rows2", [P, R, F])
        unused = sb("unused", [P, 2, CCOLS], bf16)
        ident = sb("ident", [P, P])
        spread = sb("spread", [P, (2 * QN - 1) * Q])
        w_t = sb("w_t", [P, F])
        b_bc = sb("b_bc", [P, F])
        part_p = sb("part_p", [P, R, PCH[0] // 2])
        part_d = sb("part_d", [P, RB, DCH[0]])
        sum_d = sb("sum_d", [P, RB])
        sum_p = sb("sum_p", [P, R])
        deg = sb("deg", [P, R])
        sqrt_deg = sb("sqrt_deg", [P, R])
        dinv_all = sb("dinv_all", [P, BLOCKS * R])
        dinv = sb("dinv", [P, R])
        dinv2 = sb("dinv2", [P, R])
        stats = sb("stats", [P, R, 6])
        mv = sb("mv", [P, R, 2])
        std = sb("std", [P, R])
        rstd = sb("rstd", [P, R])
        carrier = sb("carrier", [P, 1])

        a_ps = [pb(f"a_ps{i}", [P, PAIR * ROWS]) for i in range(2)]
        acc_head = pb("acc_head", [P, ROWS])
        acc_tail = pb("acc_tail", [P, ROWS])
        row_ps = pb("row_ps", [P, ROWS])
        x1_ps = pb("x1_ps", [P, ROWS])

        loaded = [sem(f"loaded{i}") for i in range(SLOTS)]
        staged = [sem(f"staged{i}") for i in range(PARTS)]
        w_loaded = sem("w_loaded")
        b_loaded = sem("b_loaded")
        zeroed = sem("zeroed")
        consts_ready = sem("consts_ready")
        w_trans = sem("w_trans")
        w_ready = sem("w_ready")
        sh_ready = sem("sh_ready")
        sl_ready = sem("sl_ready")
        tr_p = sem("tr_p")
        tr_d = sem("tr_d")
        hi_ready = sem("hi_ready")
        lo_p = sem("lo_p")
        lo_d = sem("lo_d")
        multiplied = sem("multiplied")
        folded = sem("folded")
        summed_p = sem("summed_p")
        summed_d = sem("summed_d")
        parts_read = sem("parts_read")
        across_done = sem("across_done")
        deg_ready = sem("deg_ready")
        sqrt_ready = sem("sqrt_ready")
        dinv_ready = sem("dinv_ready")
        head_out = sem("head_out")
        tail_out = sem("tail_out")
        y_ready = sem("y_ready")
        rows_loaded = sem("rows_loaded")
        mv_ready = sem("mv_ready")
        var_ready = sem("var_ready")
        std_ready = sem("std_ready")
        rstd_ready = sem("rstd_ready")
        x1_ready = sem("x1_ready")
        x1_trans = sem("x1_trans")
        x1t_ready = sem("x1t_ready")
        p_ready = sem("p_ready")
        u_ready = sem("u_ready")
        u_stored = sem("u_stored")
        uh_ready = sem("uh_ready")
        ul_ready = sem("ul_ready")
        bias_added = sem("bias_added")
        rows_done = sem("rows_done")
        rows_stored = sem("rows_stored")
        chain = sem("chain")

        block = ctx.enter_context(nc.Block())

        def wait_chunk_loaded(eng, g, ps, c):
            i = c % SLOTS
            before = sum(per_slot(k) for k, _, _ in PASSES[ps][1][i:c:SLOTS])
            eng.wait_ge(loaded[i], base(g, [n[i] for n in SLOT_INC], ps) + before + per_slot(PASSES[ps][1][c][0]))

        def wait_chunk_free(eng, g, ps, c):
            kind, n, _ = PASSES[ps][1][c]
            if kind == "P":
                tiles = SPC * PAIR
                if ps == 0:
                    gone = base(g, NPT, ps) + (n // 2 + 1) * 2 * tiles
                    eng.wait_ge(tr_p, gone)
                    eng.wait_ge(summed_p, gone)
                else:
                    eng.wait_ge(tr_p, base(g, NPT, ps) + (n + 1) * tiles)
            elif ps == 0:
                eng.wait_ge(summed_d, base(g, DCH, ps) + n + 1)
            else:
                eng.wait_ge(tr_d, base(g, NBLOCKY, ps) + (n + 1) * SPC)

        def load_d(eng, row_block, ps, c, quadrants):
            i, n = c % SLOTS, PASSES[ps][1][c][1]
            for q in quadrants:
                col = q * DQ[ps] + n * QCOLS
                eng.dma_start(chunk[q * Q:(q + 1) * Q, i, :].rearrange("c (b k) -> c b k", k=QCOLS),
                              adj_d[row_block, :, :, col:col + QCOLS]).then_inc(loaded[i], 16)

        SP_QUADRANTS, ACT_QUADRANTS = (0, 1), (2, 3)

        def d_view(slot):
            return chunk[:, slot, :].rearrange("p (b k) -> p b k", k=QCOLS)

        def p_view(slot):
            return chunk[:, slot, :].rearrange("p (r k) -> p r k", k=CCOLS)

        def part_view(ps, part):
            return chunk[:, STAGE_CHUNK[ps][part] % SLOTS, :].rearrange("p (t f) -> p t f", f=F)

        def part_tiles(ps, part):
            return U_LAST if ps == 1 and part == 0 else XT

        def staged_count(ps, part):
            return 16 * sum(QN if CONTENT[i][part][0] == "D" else 1 for i in range(ps + 1))

        @block.sync
        def _(sp):
            def stage(ps, part, source):
                (kind, first), n = CONTENT[ps][part], part_tiles(ps, part)
                if kind == "P":
                    row = DCOLS[ps] + first * P
                    sp.dma_start(part_view(ps, part)[:, 0:n, :],
                                 source[row:row + n * P, :].rearrange("(t p) f -> p t f", p=P)
                                 ).then_inc(staged[part], 16)
                else:
                    for q in range(QN):
                        row = q * DQ[ps] + first * Q
                        sp.dma_start(part_view(ps, part)[q * Q:(q + 1) * Q, 0:n, :],
                                     source[row:row + n * Q, :].rearrange("(t a) f -> a t f", a=Q)
                                     ).then_inc(staged[part], 16)

            def load_chunk(g, row_block, ps, c):
                kind, n, _ = PASSES[ps][1][c]
                if kind == "D":
                    load_d(sp, row_block, ps, c, SP_QUADRANTS)
                else:
                    col = DCOLS[ps] + n * CCOLS
                    sp.dma_start(p_view(c % SLOTS), adj_p[row_block, :, :, col:col + CCOLS]
                                 ).then_inc(loaded[c % SLOTS], 16)

            def load_rows(row_block, second):
                if second:
                    sp.dma_start(rows[:, :, :], resid[row_block]).then_inc(rows_loaded, 16)
                else:
                    sp.dma_start(rows[:, :, :], h_v[row_block]).then_inc(rows_loaded, 16)
                    sp.dma_start(rows2[:, :, :], x_v[row_block]).then_inc(rows_loaded, 16)

            def store_rows(g, row_block, second):
                sp.wait_ge(rows_done, 16 * g)
                sp.dma_start((out_v if second else resid)[row_block], rows[:, :, :]).then_inc(rows_stored, 16)

            def store_u(g, row_block):
                sp.wait_ge(u_ready, 16 * g)
                sp.dma_start(u_v[row_block], rows2[:, :, :]).then_inc(u_stored, 16)

            def run_block(g, ps, row_work):
                opening = isinstance(g, int) and g in (0, BLOCKS)
                row_block = g - BLOCKS * ps
                done = g - 1 if row_work != "second" else g - 1 - BLOCKS
                for c in range(CHUNKS):
                    for part, before in zip(PART_ORDER[ps], STAGE_BEFORE[ps]):
                        if opening and c == before:
                            into = STAGE_CHUNK[ps][part]
                            if into >= SLOTS:
                                wait_chunk_free(sp, g, ps, into - SLOTS)
                            elif ps == 1:
                                wait_chunk_free(sp, g - 1, 0, into + SLOTS)
                            if ps == 1:
                                if part == 2:
                                    sp.wait_ge(u_stored, 16 * (BLOCKS - 2))
                                else:
                                    sp.wait_ge(u_stored, 16 * (BLOCKS - 1))
                            stage(ps, part, x if ps == 0 else u_dram)
                    if opening and c in STAGE_CHUNK[ps]:
                        sp.wait_ge(sl_ready, PARTS * ps + PART_ORDER[ps].index(STAGE_CHUNK[ps].index(c)) + 1)
                    elif c >= SLOTS:
                        wait_chunk_free(sp, g, ps, c - SLOTS)
                    elif not (isinstance(g, int) and g == 0):
                        wait_chunk_free(sp, g - 1, 0 if opening else ps, c + SLOTS)
                    load_chunk(g, row_block, ps, c)
                    if row_work and c == 5:
                        if not (isinstance(g, int) and g == 1):
                            sp.wait_ge(rows_stored, 16 * (g - 1))
                            if row_work != "second":
                                sp.wait_ge(u_stored, 16 * (g - 1))
                        load_rows(done, row_work == "second")
                    if row_work and c == CHUNKS - 2:
                        store_rows(g, done, row_work == "second")
                        if row_work == "first":
                            store_u(g, done)

            sp.dma_start(feat[:, 0:F], W[:, :]).then_inc(w_loaded, 16)
            sp.dma_start(b_bc[:, :], b.rearrange("(o f) -> o f", o=1).broadcast_to([P, F])).then_inc(b_loaded, 16)
            run_block(0, 0, None)
            run_block(1, 0, "first")
            with sp.Fori(2, BLOCKS) as g:
                run_block(g, 0, "first")
            run_block(BLOCKS, 1, "last of first")
            with sp.Fori(BLOCKS + 1, ALL) as g:
                run_block(g, 1, "second")
            sp.wait_ge(rows_stored, 16 * (ALL - 1))
            load_rows(BLOCKS - 1, True)
            store_rows(ALL, BLOCKS - 1, True)
            sp.wait_ge(rows_stored, 16 * ALL)

        @block.gpsimd
        def _(pool):
            nc.gpsimd.memset(ident[:, :], 0.0).then_inc(zeroed, 1)
            nc.gpsimd.memset(spread[:, :], 0.0).then_inc(zeroed, 1)
            pool.wait_ge(zeroed, 2)
            nc.gpsimd.affine_select(out=ident[:, :], in_=ident[:, :], compare_op=ALU.not_equal, fill=1.0,
                                    base=0, pattern=[[-1, P]], channel_multiplier=1).then_inc(consts_ready, 1)
            middle = spread[:, (QN - 1) * Q:QN * Q]
            for q in range(QN):
                ins = nc.gpsimd.affine_select(out=middle, in_=middle, compare_op=ALU.not_equal, fill=1.0,
                                              base=-q * Q, pattern=[[-1, Q]], channel_multiplier=1)
                ins.then_inc(zeroed, 1)
                pool.wait_ge(zeroed, 3 + q)
                if q == QN - 1:
                    nc.gpsimd.memset(unused[:, 0:1], 0.0).then_inc(consts_ready, 1)

            def make_lo(g, s, entry, ps):
                pool.wait_ge(hi_ready, g * STEPS + s + 1)
                if not in_first(g, s - LOS):
                    pool.wait_ge(multiplied, g * STEPS + s - LOS + 1)
                nc.gpsimd.tensor_tensor(a_lo[:, s % LOS, :], a_tr[:, entry.d % TRS, :],
                                        a_hi[:, s % HIS, :].bitcast(fp32), ALU.subtract).then_inc(lo_d, 1)

            def fold_chunk(g, n, c):
                wait_chunk_loaded(pool, g, 0, c)
                if not in_first(g, n - 1):
                    pool.wait_ge(summed_d, base(g, DCH, 0) + n)
                v = d_view(c % SLOTS)
                nc.gpsimd.tensor_tensor(fold[:, :, :], v[:, :, 0:FOLD], v[:, :, FOLD:QCOLS],
                                        ALU.add).then_inc(folded, 1)

            def run_slot(g, t, ps):
                todo = ahead(g, t, LEAD_LO, ps)
                if todo and todo[2].kind == "D":
                    make_lo(*todo, ps)
                if ps == 0 and t >= 0 and t % 4 == 0 and t // 4 in FOLDED:
                    fold_chunk(g, t // 4, t // 2)

            def run_block(g, ps):
                for t in range(STEPS):
                    run_slot(g, t, ps)

            for t in range(-LEAD_LO, 0):
                run_slot(0, t, 0)
            run_block(0, 0)
            with pool.Fori(1, BLOCKS) as g:
                run_block(g, 0)
            with pool.Fori(BLOCKS, ALL - 1) as g:
                run_block(g, 1)
            run_block(ALL - 1, 1)

        @block.tensor
        def _(pe):
            def transpose_step(g, s, entry, ps):
                c = entry.chunk
                if entry.place == 0:
                    wait_chunk_loaded(pe, g, ps, c)
                if not in_first(g, entry.ps - 2):
                    pe.wait_ge(lo_p, base(g, NPS, ps) + entry.ps - 1)
                for t in range(PAIR):
                    col = (entry.place * PAIR + t) * P
                    for r in range(R):
                        last = nc.tensor.transpose(a_ps[entry.ps % 2][:, (t * R + r) * P:(t * R + r + 1) * P],
                                                   p_view(c % SLOTS)[:, r, col:col + P], ident[:, :])
                last.then_inc(tr_p, PAIR)

            def multiply_step(g, s, ps):
                entry = PASSES[ps][0][s]
                acc = acc_head if s < HEAD else acc_tail
                first, final = s in (0, HEAD), s in (HEAD - 1, STEPS - 1)
                tile = stationary(ps, s)
                pe.wait_ge(hi_ready, g * STEPS + s + 1)
                for t in range(PAIR):
                    moving = a_hi[:, s % HIS, t * ROWS:(t + 1) * ROWS]
                    nc.tensor.matmul(acc[:, :], s_hi[:, tile + t, :], moving, start=first and t == 0, stop=False)
                    nc.tensor.matmul(acc[:, :], s_lo[:, tile + t, :], moving, start=False, stop=False)
                todo = ahead(g, s, LEAD_P, ps)
                if todo and todo[2].kind == "P":
                    transpose_step(*todo, ps)
                if entry.kind == "D":
                    pe.wait_ge(lo_d, base(g, ND, ps) + entry.d + 1)
                else:
                    pe.wait_ge(lo_p, base(g, NPS, ps) + entry.ps + 1)
                for t in range(PAIR):
                    last = nc.tensor.matmul(acc[:, :], s_hi[:, tile + t, :],
                                            a_lo[:, s % LOS, t * ROWS:(t + 1) * ROWS],
                                            start=False, stop=final and t == PAIR - 1)
                last.then_inc(multiplied, 1)

            def row_sums_across(g):
                pe.wait_ge(parts_read, g)
                for v in range(QN):
                    last = nc.tensor.matmul(x1_ps[:, 0:R], spread[:, (QN - 1 - v) * Q:(2 * QN - 1 - v) * Q],
                                            sum_d[:, v:RB:QN], start=v == 0, stop=v == QN - 1)
                last.then_inc(across_done, 1)

            def rows_back(g):
                pe.wait_ge(tail_out, g)
                for r in range(R):
                    last = nc.tensor.transpose(row_ps[:, r * P:(r + 1) * P], feat[:, r * P:(r + 1) * P], ident[:, :])
                last.then_inc(y_ready, 1)

            def x1_transpose(g):
                pe.wait_ge(x1_ready, g)
                for r in range(R):
                    last = nc.tensor.transpose(x1_ps[:, r * P:(r + 1) * P], rows[:, r, :], ident[:, :])
                last.then_inc(x1_trans, 1)

            def x1_weights(g):
                pe.wait_ge(x1t_ready, g)
                for r in range(R):
                    last = nc.tensor.matmul(row_ps[:, r * P:(r + 1) * P], feat[:, r * P:(r + 1) * P], w_t[:, :],
                                            start=True, stop=True)
                last.then_inc(p_ready, 1)

            def run_block(g, ps, row_work):
                opening = isinstance(g, int) and g in (0, BLOCKS)
                seen = 0
                for s in range(STEPS):
                    if opening:
                        need = PART_ORDER[ps].index(stationary(ps, s) // XT) + 1
                        if need > seen:
                            pe.wait_ge(sl_ready, PARTS * ps + need)
                            seen = need
                    if opening and ps == 1 and s == STEPS - SPC:
                        pe.wait_ge(ul_ready, 1)
                    if row_work and s == 0:
                        pe.wait_ge(head_out, g)
                    if row_work and s == HEAD:
                        pe.wait_ge(tail_out, g)
                    multiply_step(g, s, ps)
                    if row_work and row_work != "second" and s == 2:
                        row_sums_across(g)
                    if row_work and s == 4:
                        rows_back(g)
                    if row_work and row_work != "second" and s == 13:
                        x1_transpose(g)
                    if row_work and row_work != "second" and s == 16:
                        x1_weights(g)

            pe.wait_ge(consts_ready, 2)
            pe.wait_ge(w_loaded, 16)
            nc.tensor.transpose(row_ps[:, 0:F], feat[:, 0:F], ident[:, :]).then_inc(w_trans, 1)
            for t in range(-LEAD_P, 0):
                todo = ahead(0, t, LEAD_P, 0)
                if todo[2].kind == "P":
                    transpose_step(*todo, 0)
            pe.wait_ge(w_ready, 1)
            run_block(0, 0, None)
            with pe.Fori(1, BLOCKS) as g:
                run_block(g, 0, "first")
            run_block(BLOCKS, 1, "last of first")
            with pe.Fori(BLOCKS + 1, ALL - 1) as g:
                run_block(g, 1, "second")
            run_block(ALL - 1, 1, "second")
            rows_back(ALL)

        @block.scalar
        def _(act):
            def make_hi(g, s, entry, ps):
                if entry.kind == "P":
                    act.wait_ge(tr_p, base(g, NPT, ps) + (entry.p + 1) * PAIR)
                else:
                    act.wait_ge(tr_d, base(g, NBLOCKY, ps) + entry.blocky + 1)
                source = a_tr[:, entry.d % TRS, :] if entry.kind == "D" else a_ps[entry.ps % 2][:, :]
                if not in_first(g, s - HIS):
                    act.wait_ge(multiplied, g * STEPS + s - HIS + 1)
                nc.scalar.activation(a_hi[:, s % HIS, :], source, ACT.Copy).then_inc(hi_ready, 1)

            def sum_pair(g, pair, r):
                c = 4 * pair + 1
                if r == 0:
                    wait_chunk_loaded(act, g, 0, c)
                    wait_chunk_loaded(act, g, 0, c + 2)
                    if pair == 0 and not in_first(g, -1):
                        act.wait_ge(parts_read, g)
                if not in_first(g, pair * R + r - 1):
                    act.wait_ge(summed_p, base(g, NPT, 0) + 2 * (pair * R + r))
                both = chunk[:, c % SLOTS:c % SLOTS + 3:2, r * CCOLS:(r + 1) * CCOLS]
                nc.scalar.activation(unused[:, :, :], both, ACT.Copy,
                                     accum_out=part_p[:, r, pair:pair + 1]).then_inc(summed_p, 2)

            def root_degrees(g):
                act.wait_ge(deg_ready, g)
                nc.scalar.activation(sqrt_deg[:, :], deg[:, :], ACT.Sqrt).then_inc(sqrt_ready, 1)

            def deviation(g):
                act.wait_ge(var_ready, g)
                nc.scalar.activation(std[:, :], std[:, :], ACT.Sqrt).then_inc(std_ready, 1)

            def x1_copy(g):
                act.wait_ge(x1_trans, g)
                nc.scalar.activation(feat[:, :], x1_ps[:, :], ACT.Copy).then_inc(x1t_ready, 1)

            def make_u(g, last_block):
                act.wait_ge(p_ready, g)
                act.wait_ge(dinv_ready, g)
                for r in range(R):
                    to = s_hi[:, U_LAST + r, :] if last_block else rows2[:, r, :]
                    last = nc.scalar.activation(to, row_ps[:, r * P:(r + 1) * P], ACT.Copy, scale=dinv[:, r:r + 1])
                if last_block:
                    last.then_inc(uh_ready, 1)
                else:
                    last.then_inc(u_ready, 16)

            def take_head(g, row_work):
                if row_work == "second":
                    act.wait_ge(y_ready, g)
                elif row_work:
                    act.wait_ge(p_ready, g)
                act.wait_ge(multiplied, g * STEPS + HEAD)
                nc.scalar.activation(feat[:, :], acc_head[:, :], ACT.Copy).then_inc(head_out, 1)

            def split_part(ps, i):
                part = PART_ORDER[ps][i]
                n = part_tiles(ps, part)
                act.wait_ge(staged[part], staged_count(ps, part))
                if ps == 1:
                    act.wait_ge(multiplied, BLOCKS * STEPS - (STEPS // 2 if i < 2 else 0))
                nc.scalar.activation(s_hi[:, part * XT:part * XT + n, :], part_view(ps, part)[:, 0:n, :],
                                     ACT.Copy).then_inc(sh_ready, 1)

            def free_at(ps, c):
                kind, _, last = PASSES[ps][1][c]
                if ps == 1:
                    return last
                return last + 4 if kind == "D" else last + 6

            def load_slot(g, t, ps, ps_before, ps_next):
                for c in range(CHUNKS):
                    if PASSES[ps][1][c][0] != "D" or ps_before != ps and c in STAGE_CHUNK[ps]:
                        continue
                    if c >= SLOTS:
                        if free_at(ps, c - SLOTS) == t:
                            wait_chunk_free(act, g, ps, c - SLOTS)
                            load_d(act, g - BLOCKS * ps, ps, c, ACT_QUADRANTS)
                    elif ps_before is None:
                        continue
                    elif free_at(ps_before, c + SLOTS) - STEPS == t:
                        wait_chunk_free(act, g - 1, ps_before, c + SLOTS)
                        load_d(act, g - BLOCKS * ps, ps, c, ACT_QUADRANTS)
                if ps_next is None:
                    return
                for c in range(SLOTS):
                    if ps_next != ps and c in STAGE_CHUNK[ps_next]:
                        continue
                    if PASSES[ps_next][1][c][0] == "D" and free_at(ps, c + SLOTS) == t:
                        wait_chunk_free(act, g, ps, c + SLOTS)
                        load_d(act, g + 1 - BLOCKS * ps_next, ps_next, c, ACT_QUADRANTS)

            def load_after_split(ps, i):
                c = STAGE_CHUNK[ps][PART_ORDER[ps][i]]
                if PASSES[ps][1][c][0] == "D":
                    act.wait_ge(sl_ready, PARTS * ps + i + 1)
                    load_d(act, 0, ps, c, ACT_QUADRANTS)

            def run_slot(g, t, ps):
                todo = ahead(g, t, LEAD_HI, ps)
                if todo:
                    make_hi(*todo, ps)

            def run_block(g, ps, row_work, ps_before, ps_next):
                opening = isinstance(g, int) and g in (0, BLOCKS)
                for t in range(STEPS):
                    run_slot(g, t, ps)
                    if opening and t in SPLIT_LAST[ps]:
                        split_part(ps, 2 + SPLIT_LAST[ps].index(t))
                    if opening and t - 2 in SPLIT_LAST[ps]:
                        load_after_split(ps, 2 + SPLIT_LAST[ps].index(t - 2))
                    if isinstance(g, int) and g == BLOCKS - 1:
                        if t in SPLIT_U:
                            split_part(1, SPLIT_U.index(t))
                        if t - 2 in SPLIT_U:
                            load_after_split(1, SPLIT_U.index(t - 2))
                    if ps == 0 and t % 2 == 1:
                        sum_pair(g, t // 8, t % 8 // 2)
                    if row_work and row_work != "second":
                        if t == 6:
                            root_degrees(g)
                        if t == 15:
                            x1_copy(g)
                        if t == 18:
                            make_u(g, row_work == "last of first")
                    if row_work and t == 10:
                        deviation(g)
                    if t == 22:
                        take_head(g, row_work)
                    load_slot(g, t, ps, ps_before, ps_next)

            load_d(act, 0, 0, 0, ACT_QUADRANTS)
            act.wait_ge(consts_ready, 2)
            nc.scalar.activation(std[:, :], ident[:, 0:R], ACT.Sqrt)
            act.wait_ge(w_trans, 1)
            nc.scalar.activation(w_t[:, :], row_ps[:, 0:F], ACT.Copy).then_inc(w_ready, 1)
            load_d(act, 0, 0, 2, ACT_QUADRANTS)
            for t in range(-LEAD_HI, 0):
                run_slot(0, t, 0)
                if t == -LEAD_HI:
                    for c in (4, 6):
                        load_d(act, 0, 0, c, ACT_QUADRANTS)
                if t + LEAD_HI < 2:
                    split_part(0, t + LEAD_HI)
            run_block(0, 0, None, None, 0)
            with act.Fori(1, BLOCKS - 1) as g:
                run_block(g, 0, "first", 0, 0)
            run_block(BLOCKS - 1, 0, "first", 0, 1)
            run_block(BLOCKS, 1, "last of first", 0, 1)
            with act.Fori(BLOCKS + 1, ALL - 1) as g:
                run_block(g, 1, "second", 1, 1)
            run_block(ALL - 1, 1, "second", 1, None)
            deviation(ALL)

        @block.vector
        def _(dve):
            CHAIN = (5, 3)

            def link(ins):
                return ins.then_inc(chain, 1)

            def transpose_step(g, s, entry, ps):
                c = entry.chunk
                if entry.place == 0:
                    wait_chunk_loaded(dve, g, ps, c)
                if entry.kind == "D":
                    to = a_tr[:, entry.d % TRS, :]
                    if not in_first(g, entry.d - TRS):
                        dve.wait_ge(lo_d, used_before(g, entry.d, TRS, ND, ps))
                else:
                    to = a_ps[entry.ps % 2][:, :]
                    if not in_first(g, entry.ps - 2):
                        dve.wait_ge(lo_p, base(g, NPS, ps) + entry.ps - 1)
                col = entry.place * PAIR * Q
                source = d_view(c % SLOTS)[:, :, col:col + PAIR * Q].rearrange("p b (t a) -> p t b a", a=Q)
                nc.vector.transpose(to, source).then_inc(tr_d, 1)

            def make_lo(g, s, entry, ps):
                dve.wait_ge(hi_ready, g * STEPS + s + 1)
                if not in_first(g, s - LOS):
                    dve.wait_ge(multiplied, g * STEPS + s - LOS + 1)
                nc.vector.tensor_tensor(a_lo[:, s % LOS, :], a_ps[entry.ps % 2][:, :],
                                        a_hi[:, s % HIS, :].bitcast(fp32), ALU.subtract).then_inc(lo_p, 1)

            def sum_chunk(g, n, c, half):
                b = slice(half * HALF, (half + 1) * HALF)
                if n == 0 and half == 0 and not in_first(g, -1):
                    dve.wait_ge(parts_read, g)
                if n in FOLDED:
                    dve.wait_ge(folded, g * len(FOLDED) + FOLDED.index(n) + 1)
                    source = fold[:, b, :]
                else:
                    source = d_view(c % SLOTS)[:, b, :]
                last = nc.vector.tensor_reduce(part_d[:, b, n:n + 1], source, AX.X, ALU.add)
                if half == 1:
                    last.then_inc(summed_d, 1)

            def sum_parts(g):
                dve.wait_ge(summed_p, base(g, NPT, 0))
                dve.wait_ge(summed_d, base(g, DCH, 0))
                link(nc.vector.tensor_reduce(sum_p[:, :], part_p[:, :, :], AX.X, ALU.add))
                nc.vector.tensor_reduce(sum_d[:, :], part_d[:, :, :], AX.X, ALU.add).then_inc(parts_read, 1)

            def degrees(g, at):
                dve.wait_ge(chain, at + 1)
                dve.wait_ge(across_done, g)
                link(nc.vector.tensor_tensor(deg[:, :], x1_ps[:, 0:R], sum_p[:, :], ALU.add))
                dve.wait_ge(chain, at + 2)
                nc.vector.tensor_scalar(deg[:, :], deg[:, :], 1.0, None, ALU.add).then_inc(deg_ready, 1)

            def inverse_degrees(g, row_block):
                dve.wait_ge(sqrt_ready, g)
                nc.vector.reciprocal(dinv[:, :], sqrt_deg[:, :])
                nc.vector.reciprocal(dinv_all[:, bass.ds(row_block * R, R)], sqrt_deg[:, :])
                nc.vector.reciprocal(dinv2[:, :], deg[:, :]).then_inc(dinv_ready, 1)

            def take_dinv(row_block, at):
                link(nc.vector.tensor_copy(dinv[:, :], dinv_all[:, bass.ds(row_block * R, R)]))

            def add_tail(g):
                dve.wait_ge(multiplied, g * STEPS)
                dve.wait_ge(head_out, g)
                nc.vector.tensor_tensor(feat[:, :], acc_tail[:, :], feat[:, :], ALU.add).then_inc(tail_out, 1)

            def mix_inputs(g):
                dve.wait_ge(rows_loaded, 32 * g)
                link(nc.vector.scalar_tensor_tensor(rows[:, :, :], rows[:, :, :], ALPHA, rows2[:, :, :],
                                                    ALU.mult, ALU.add))

            def first_rows(g, at):
                dve.wait_ge(y_ready, g)
                dve.wait_ge(chain, at + 3)
                link(nc.vector.scalar_tensor_tensor(rows[:, :, :], row_ps[:, :].rearrange("p (r f) -> p r f", f=F),
                                                    1.0 - ALPHA, rows[:, :, :], ALU.mult, ALU.add))

            def second_rows(g, at):
                dve.wait_ge(chain, at + 1)
                dve.wait_ge(y_ready, g)
                dve.wait_ge(rows_loaded, 16 * g + 16 * BLOCKS)
                for r in range(R):
                    last = nc.vector.scalar_tensor_tensor(rows[:, r, :], row_ps[:, r * P:(r + 1) * P],
                                                          dinv[:, r:r + 1], rows[:, r, :], ALU.mult, ALU.add)
                link(last)

            def statistics(seen):
                dve.wait_ge(chain, seen)
                for r in range(R):
                    last = nc.vector.bn_stats(stats[:, r, :], rows[:, r, :])
                link(last)

            def variance(seen):
                dve.wait_ge(chain, seen)
                nc.vector.memset(carrier[:, :], 0.0)
                for r in range(R):
                    last = nc.vector.bn_aggr(mv[:, r, :], stats[:, r, :])
                last.then_inc(mv_ready, 1)

            def add_eps(g):
                dve.wait_ge(mv_ready, g)
                nc.vector.tensor_scalar(std[:, :], mv[:, :, 1], EPS, None, ALU.add).then_inc(var_ready, 1)

            def inverse_deviation(g):
                dve.wait_ge(std_ready, g)
                nc.vector.reciprocal(rstd[:, :], std[:, :]).then_inc(rstd_ready, 1)

            def normalise(g, done, by):
                dve.wait_ge(rstd_ready, g)
                for r in range(R):
                    last = nc.vector.tensor_scalar(rows[:, r, :], rows[:, r, :], mv[:, r, 0:1], rstd[:, r:r + 1],
                                                   ALU.subtract, ALU.mult)
                last.then_inc(done, by)

            def last_u_low(g):
                dve.wait_ge(uh_ready, 1)
                for r in range(R):
                    last = nc.vector.scalar_tensor_tensor(s_lo[:, U_LAST + r, :], row_ps[:, r * P:(r + 1) * P],
                                                          dinv[:, r:r + 1], s_hi[:, U_LAST + r, :].bitcast(fp32),
                                                          ALU.mult, ALU.subtract)
                last.then_inc(ul_ready, 1)

            def residual_bias(g):
                dve.wait_ge(x1_trans, g)
                bias = b_bc[:, :].rearrange("p (o f) -> p o f", o=1).broadcast_to([P, R, F])
                nc.vector.tensor_tensor(rows[:, :, :], rows[:, :, :], bias, ALU.add).then_inc(bias_added, 1)

            def residual(g, last_block):
                dve.wait_ge(bias_added, g)
                if last_block:
                    dve.wait_ge(uh_ready, 1)
                else:
                    dve.wait_ge(u_ready, 16 * g)
                for r in range(R):
                    last = nc.vector.scalar_tensor_tensor(rows[:, r, :], row_ps[:, r * P:(r + 1) * P],
                                                          dinv2[:, r:r + 1], rows[:, r, :], ALU.mult, ALU.add)
                last.then_inc(rows_done, 16)

            def split_part(ps, i):
                part = PART_ORDER[ps][i]
                n = part_tiles(ps, part)
                dve.wait_ge(sh_ready, PARTS * ps + i + 1)
                nc.vector.tensor_tensor(s_lo[:, part * XT:part * XT + n, :], part_view(ps, part)[:, 0:n, :],
                                        s_hi[:, part * XT:part * XT + n, :].bitcast(fp32),
                                        ALU.subtract).then_inc(sl_ready, 1)

            def run_slot(g, t, ps):
                todo = ahead(g, t, LEAD_D, ps)
                if todo and todo[2].kind != "P":
                    transpose_step(*todo, ps)
                todo = ahead(g, t, LEAD_LO, ps)
                if todo and todo[2].kind != "D":
                    make_lo(*todo, ps)

            def first_row_work(g, t, at, last_block):
                if t == 0:
                    sum_parts(g)
                if t == 1:
                    add_tail(g)
                if t == 4:
                    degrees(g, at)
                if t == 6:
                    mix_inputs(g)
                if t == 7:
                    first_rows(g, at)
                if t == 8:
                    inverse_degrees(g, g - 1)
                    statistics(at + 4)
                if t == 9:
                    variance(at + 5)
                    add_eps(g)
                if t == 11:
                    inverse_deviation(g)
                if t == 12:
                    normalise(g, x1_ready, 1)
                if t == 16:
                    residual_bias(g)
                if t == 19 and last_block:
                    last_u_low(g)
                if t == 19:
                    residual(g, last_block)

            def second_row_work(g, t, at):
                if t == 1:
                    add_tail(g)
                if t == 3:
                    take_dinv(g - 1 - BLOCKS, at)
                if t == 7:
                    second_rows(g, at)
                if t == 8:
                    statistics(at + 2)
                if t == 9:
                    variance(at + 3)
                    add_eps(g)
                if t == 11:
                    inverse_deviation(g)
                if t == 12:
                    normalise(g, rows_done, 16)

            def run_block(g, ps, row_work):
                opening = isinstance(g, int) and g in (0, BLOCKS)
                for t in range(STEPS):
                    run_slot(g, t, ps)
                    if opening and t - 1 in SPLIT_LAST[ps]:
                        split_part(ps, 2 + SPLIT_LAST[ps].index(t - 1))
                    if isinstance(g, int) and g == BLOCKS - 1 and t - 1 in SPLIT_U:
                        split_part(1, SPLIT_U.index(t - 1))
                    if row_work in ("first", "last of first"):
                        first_row_work(g, t, (g - 1) * CHAIN[0], row_work == "last of first")
                    if row_work == "second":
                        second_row_work(g, t, BLOCKS * CHAIN[0] + (g - 1 - BLOCKS) * CHAIN[1])
                    if ps == 0:
                        n, k = t // 4, t % 4
                        if k >= 2:
                            sum_chunk(g, n, 2 * n, k - 2)

            dve.wait_ge(b_loaded, 16)
            for t in range(-LEAD_D, 0):
                if t == -2:
                    split_part(0, 0)
                    split_part(0, 1)
                run_slot(0, t, 0)
            run_block(0, 0, None)
            with dve.Fori(1, BLOCKS - 1) as g:
                run_block(g, 0, "first")
            run_block(BLOCKS - 1, 0, "first")
            run_block(BLOCKS, 1, "last of first")
            with dve.Fori(BLOCKS + 1, ALL - 1) as g:
                run_block(g, 1, "second")
            run_block(ALL - 1, 1, "second")
            for t in range(STEPS):
                second_row_work(ALL, t, BLOCKS * CHAIN[0] + (ALL - 1 - BLOCKS) * CHAIN[1])


_INS = ["x", "adj", "L0_gnn_h", "L1_gnn_W", "L1_gnn_b"]


def kernel(**inputs):
    import numpy as _np
    import concourse.bacc as _bacc
    from concourse import mybir as _mybir
    from concourse.bass_utils import run_bass_kernel_spmd as _run

    nc = _bacc.Bacc("TRN2", target_bir_lowering=False, num_devices=1)
    arrays, args = {}, []
    for name in _INS:
        a = _np.ascontiguousarray(inputs[name])
        arrays[f"in_{name}_dram"] = a
        args.append(nc.dram_tensor(f"in_{name}_dram", a.shape, _mybir.dt.from_np(a.dtype), kind="ExternalInput").ap())
    shape = tuple(inputs["x"].shape)
    args.append(nc.dram_tensor("out_dram", shape, _mybir.dt.float32, kind="ExternalOutput").ap())
    graph_resnorm_kernel(nc, *args)
    r = _run(nc, [arrays], core_ids=[0])
    return r.results[0]["out_dram"]
```
